# Optimizing a Trainium2 kernel written in Bass

```python
import numpy as np
import jax
import jax.numpy as jnp

def _softmax(x, axis=-1):
    return jax.nn.softmax(x, axis=axis)

def _gelu(x):
    return jax.nn.gelu(x, approximate=True)

def _silu(x):
    return jax.nn.silu(x)

def _sigmoid(x):
    return jax.nn.sigmoid(x)

def _layernorm(x, axis=-1, eps=1e-05):
    m = jnp.mean(x, axis=axis, keepdims=True)
    v = jnp.var(x, axis=axis, keepdims=True)
    return (x - m) / jnp.sqrt(v + eps)

def _scatter_add(tgt, idx, src, axis=0):
    return tgt.at[idx].add(src)

def _segment_sum(src, seg, n):
    return jax.ops.segment_sum(src, seg, n)
kernel_name = 'mk_adj_preln_d4_adj_r2_7ad782'

def setup_inputs(seed: int=0):
    np.random.seed(seed)
    _w = jnp.asarray

    def _rec_inputs():
        import jax
        import jax.numpy as jnp
        _gk = jax.random.key(seed)
        x = -0.0005207 + 1.001 * jax.random.normal(jax.random.fold_in(_gk, 1), (3327, 256), jnp.float32)
        _w = (1.0 + jnp.arange(3327, dtype=jnp.float32)) ** (-0.5)
        _w = _w / _w.mean()
        _pij = jnp.clip(0.00240457 * _w[:, None] * _w[None, :], 0.0, 1.0)
        _a = jax.random.uniform(jax.random.fold_in(_gk, 2), (3327, 3327)) < _pij
        _a = jnp.logical_or(_a, jnp.eye(3327, dtype=bool))
        _af = _a.astype(jnp.float32)
        _af = _af * jax.random.uniform(jax.random.fold_in(_gk, 3), (3327, 3327), jnp.float32, 0.05, 1)
        adj = _af
        return (x, adj)
    x, adj = _rec_inputs()

    def _L0_gnn_setup():
        import jax, jax.numpy as jnp
        import numpy as np
        N = 2048
        IN_F = 256
        OUT_F = 256
        key = jax.random.key(seed)
        k1, k2, k3, k4 = jax.random.split(key, 4)
        x = jax.random.normal(k1, (N, IN_F), dtype=jnp.float32)
        adj = jax.random.uniform(k2, (N, N), dtype=jnp.float32)
        bound = 1.0 / np.sqrt(IN_F)
        W = jax.random.uniform(k3, (OUT_F, IN_F), minval=-bound, maxval=bound, dtype=jnp.float32)
        b = jax.random.uniform(k4, (OUT_F,), minval=-bound, maxval=bound, dtype=jnp.float32)
        return {'x': x, 'adj': adj, 'W': W, 'b': b}
    _L0_gnn_all = _L0_gnn_setup()
    _L0_gnn_in = {k: v for k, v in _L0_gnn_all.items() if k in ('W', 'b')}
    del _L0_gnn_all

    def _L1_gnn_setup():
        import jax, jax.numpy as jnp
        import numpy as np
        N = 4096
        IN_F = 256
        OUT_F = 256
        key = jax.random.key(seed)
        k_x, k_adj, k_w = jax.random.split(key, 3)
        x = jax.random.normal(k_x, (N, IN_F), dtype=jnp.float32)
        adj = jax.random.uniform(k_adj, (N, N), dtype=jnp.float32)
        stdv = 1.0 / np.sqrt(OUT_F)
        weight = jax.random.uniform(k_w, (IN_F, OUT_F), dtype=jnp.float32, minval=-stdv, maxval=stdv)
        return {'x': x, 'adj': adj, 'weight': weight}
    _L1_gnn_all = _L1_gnn_setup()
    _L1_gnn_in = {k: v for k, v in _L1_gnn_all.items() if k in ('weight',)}
    del _L1_gnn_all

    def _L2_gnn_setup():
        import jax, jax.numpy as jnp
        import numpy as np
        N, D_IN, D_ATTN, STEPS, P_NUC, TAU = (2048, 256, 64, 2, 0.9, 1.0)
        LN_EPS = 1e-05

        def _xavier(key, shape):
            fan_in, fan_out = (shape[-2], shape[-1])
            lim = np.sqrt(6.0 / (fan_in + fan_out))
            return jax.random.uniform(key, shape, jnp.float32, -lim, lim)

        def _adj_from_feats(Xa, W1, W2, W3):
            Q = Xa @ W1
            K = Xa @ W3
            logits = Q @ W2 @ K.T / TAU
            idx = jnp.argsort(-logits, axis=1)
            vals = jnp.take_along_axis(logits, idx, axis=1)
            csum = jnp.cumsum(jax.nn.softmax(vals, axis=1), axis=1)
            k_i = jnp.sum(csum < P_NUC, axis=1) + 1
            ranks = jnp.arange(logits.shape[1])[None, :]
            keep_sorted = ranks < k_i[:, None]
            inv = jnp.argsort(idx, axis=1)
            keep = jnp.take_along_axis(keep_sorted, inv, axis=1)
            masked = jnp.where(keep, logits, -jnp.inf)
            return jax.nn.softmax(masked, axis=1)
        key = jax.random.key(seed)
        ks = jax.random.split(key, 9)
        return {'X': jax.random.normal(ks[0], (N, D_IN), jnp.float32), 'S': jax.random.uniform(ks[1], (N, N), jnp.float32), 'W1': _xavier(ks[2], (D_IN, D_ATTN)), 'W2': _xavier(ks[3], (D_ATTN, D_ATTN)), 'W3': _xavier(ks[4], (D_IN, D_ATTN)), 'U1': _xavier(ks[5], (STEPS, D_IN, D_IN)), 'U2': _xavier(ks[6], (STEPS, D_IN, D_IN)), 'U3': _xavier(ks[7], (STEPS, D_IN, D_IN)), 'gamma': jnp.ones((D_IN,), jnp.float32), 'beta': jnp.zeros((D_IN,), jnp.float32)}
    _L2_gnn_all = _L2_gnn_setup()
    _L2_gnn_in = {k: v for k, v in _L2_gnn_all.items() if k in ('W1', 'W2', 'W3', 'U1', 'U2', 'U3', 'gamma', 'beta')}
    del _L2_gnn_all

    def _L3_gnn_setup():
        import jax, jax.numpy as jnp
        import numpy as np
        N = 5000
        IN_F = 256
        OUT_F = 256
        key = jax.random.key(seed)
        k1, k2, k3 = jax.random.split(key, 3)
        x = jax.random.normal(k1, (N, IN_F), dtype=jnp.float32)
        adj = jax.random.uniform(k2, (N, N), dtype=jnp.float32)
        stdv = 1.0 / np.sqrt(OUT_F)
        weight = jax.random.uniform(k3, (IN_F, OUT_F), dtype=jnp.float32, minval=-stdv, maxval=stdv)
        t = jnp.ones((1,), dtype=jnp.float32)
        return {'x': x, 'adj': adj, 't': t, 'weight': weight}
    _L3_gnn_all = _L3_gnn_setup()
    _L3_gnn_in = {k: v for k, v in _L3_gnn_all.items() if k in ('t', 'weight')}
    del _L3_gnn_all
    return {'x': x, 'adj': adj, 'L0_gnn_W': _L0_gnn_in['W'], 'L0_gnn_b': _L0_gnn_in['b'], 'L1_gnn_weight': _L1_gnn_in['weight'], 'L2_gnn_W1': _L2_gnn_in['W1'], 'L2_gnn_W2': _L2_gnn_in['W2'], 'L2_gnn_W3': _L2_gnn_in['W3'], 'L2_gnn_U1': _L2_gnn_in['U1'], 'L2_gnn_U2': _L2_gnn_in['U2'], 'L2_gnn_U3': _L2_gnn_in['U3'], 'L2_gnn_gamma': _L2_gnn_in['gamma'], 'L2_gnn_beta': _L2_gnn_in['beta'], 'L3_gnn_t': _L3_gnn_in['t'], 'L3_gnn_weight': _L3_gnn_in['weight']}

def reference(x, adj, L0_gnn_W, L0_gnn_b, L1_gnn_weight, L2_gnn_W1, L2_gnn_W2, L2_gnn_W3, L2_gnn_U1, L2_gnn_U2, L2_gnn_U3, L2_gnn_gamma, L2_gnn_beta, L3_gnn_t, L3_gnn_weight):
    import jax
    import jax.numpy as jnp

    def _L0_gnn_ref(x, adj, W, b):
        import jax, jax.numpy as jnp
        import numpy as np
        N = 2048
        IN_F = 256
        OUT_F = 256
        adj_hat = adj + jnp.eye(adj.shape[0], dtype=adj.dtype)
        d = 1.0 / jnp.sqrt(adj_hat.sum(axis=1))
        norm_adj = d[:, None] * adj_hat * d[None, :]
        h = norm_adj @ x
        return h @ W.T + b

    def _L1_gnn_ref(x, adj, weight):
        import jax, jax.numpy as jnp
        import numpy as np
        N = 4096
        IN_F = 256
        OUT_F = 256
        n = adj.shape[0]
        adj_hat = adj + jnp.eye(n, dtype=adj.dtype)
        rowsum = adj_hat.sum(axis=1)
        d_inv_sqrt = jnp.power(rowsum, -0.5)
        d_inv_sqrt = jnp.where(jnp.isinf(d_inv_sqrt), 0.0, d_inv_sqrt)
        adj_norm = adj_hat * d_inv_sqrt[:, None] * d_inv_sqrt[None, :]
        support = x @ weight
        out = adj_norm @ support
        return jax.nn.relu(out)

    def _L2_gnn_ref(X, S, W1, W2, W3, U1, U2, U3, gamma, beta):
        import jax, jax.numpy as jnp
        import numpy as np
        N, D_IN, D_ATTN, STEPS, P_NUC, TAU = (2048, 256, 64, 2, 0.9, 1.0)
        LN_EPS = 1e-05

        def _xavier(key, shape):
            fan_in, fan_out = (shape[-2], shape[-1])
            lim = np.sqrt(6.0 / (fan_in + fan_out))
            return jax.random.uniform(key, shape, jnp.float32, -lim, lim)

        def _adj_from_feats(Xa, W1, W2, W3):
            Q = Xa @ W1
            K = Xa @ W3
            logits = Q @ W2 @ K.T / TAU
            idx = jnp.argsort(-logits, axis=1)
            vals = jnp.take_along_axis(logits, idx, axis=1)
            csum = jnp.cumsum(jax.nn.softmax(vals, axis=1), axis=1)
            k_i = jnp.sum(csum < P_NUC, axis=1) + 1
            ranks = jnp.arange(logits.shape[1])[None, :]
            keep_sorted = ranks < k_i[:, None]
            inv = jnp.argsort(idx, axis=1)
            keep = jnp.take_along_axis(keep_sorted, inv, axis=1)
            masked = jnp.where(keep, logits, -jnp.inf)
            return jax.nn.softmax(masked, axis=1)
        n = X.shape[0]
        S = S + jnp.eye(n, dtype=X.dtype)
        Rf = S / jnp.clip(S.sum(axis=1, keepdims=True), 1e-12)
        Rb = S / jnp.clip(S.sum(axis=0), 1e-12)[:, None]
        Xf, Xb, Xa = (X, X, X)
        Z = jnp.zeros_like(X)
        for s in range(STEPS):
            A = _adj_from_feats(Xa, W1, W2, W3)
            Xf = Rf @ Xf
            Xb = Rb @ Xb
            Xa = A @ Xa
            Z = Z + (Xf @ U1[s] + Xb @ U2[s] + Xa @ U3[s])
        Y = X + Z
        mu = Y.mean(axis=-1, keepdims=True)
        var = Y.var(axis=-1, keepdims=True)
        return (Y - mu) / jnp.sqrt(var + LN_EPS) * gamma + beta

    def _L3_gnn_ref(x, adj, t, weight):
        import jax, jax.numpy as jnp
        import numpy as np
        N = 5000
        IN_F = 256
        OUT_F = 256
        ts = t[0]
        support = x @ weight
        return (1.0 - ts) * support + ts * (adj @ support)
    h = jnp.maximum(_layernorm(x, axis=-1), 0.0)
    x = x + _L0_gnn_ref(h, adj, L0_gnn_W, L0_gnn_b)
    h = jnp.maximum(_layernorm(x, axis=-1), 0.0)
    x = x + _L1_gnn_ref(h, adj, L1_gnn_weight)
    h = jnp.maximum(_layernorm(x, axis=-1), 0.0)
    x = x + _L2_gnn_ref(h, adj, L2_gnn_W1, L2_gnn_W2, L2_gnn_W3, L2_gnn_U1, L2_gnn_U2, L2_gnn_U3, L2_gnn_gamma, L2_gnn_beta)
    h = jnp.maximum(_layernorm(x, axis=-1), 0.0)
    x = x + _L3_gnn_ref(h, adj, L3_gnn_t, L3_gnn_weight)
    return x

_drawn_inputs = setup_inputs


def setup_inputs(seed=0):
    import zlib

    import numpy as np

    out = dict(_drawn_inputs(seed))
    spreads = {'L2_gnn_gamma': (1.0, 0.2), 'L2_gnn_beta': (0.0, 0.1)}
    factors = {}
    for name, (base, spread) in spreads.items():
        noise = np.random.default_rng([zlib.crc32(name.encode()), seed]).standard_normal(out[name].shape)
        drawn = base * np.exp(spread * noise) if base else spread * noise
        out[name] = jnp.asarray(drawn.astype(out[name].dtype))
    for name, factor in factors.items():
        out[name] = (out[name] * factor).astype(out[name].dtype)
    return out
```

```python
from contextlib import ExitStack, contextmanager

import numpy as np
import concourse.bass as bass
from concourse import mybir

F32 = mybir.dt.float32
I32 = mybir.dt.int32
ALU = mybir.AluOpType
ACT = mybir.ActivationFunctionType
AX_X = mybir.AxisListType.X

P = 128
LN_EPS = 1e-5
CLIP = 1e-12
P_NUC = 0.9
TOP = 8
EVALS = (5, 6)
AIM = 3.0
KEEP_END = 0.8
FIRST_GUESS = 0.02
MARK_PAD = 5.0
MARKED = -1.0


@contextmanager
def phase_semaphores(nc, prefix=""):
    mine = []

    def new(name):
        mine.append(nc.alloc_semaphore(prefix + name))
        return mine[-1]
    yield new
    nc.clear_and_free_semaphores(mine)
    nc.all_engine_barrier()


def pipeline(eng, tiles, body, depth=2, lead=4):
    def static(u):
        body(u, u % 2, [0 <= u - k < tiles for k in range(depth + 1)])
    for u in range(lead):
        static(u)
    if tiles > lead:
        with eng.Fori(lead, tiles - 1, 2) as u:
            body(u, 0, [True] * (depth + 1))
            body(u + 1, 1, [True] * (depth + 1))
    for u in range(tiles, tiles + depth):
        static(u)


def build(nc, n_nodes, xin, adjT, W0T, b0, W1g, A1T, A2, A3, UA, UB, UC, gamma, beta, tin, Wg3, out):
    N = n_nodes
    NT = xin.shape[0] // P
    NP = NT * P
    D = xin.shape[1]
    DC = D // P
    A = A2.shape[0]
    CW = 512
    CHUNKS = [(c, min(CW, NP - c)) for c in range(0, NP, CW)]
    KC = len(CHUNKS)
    assert NT % 2 == 0 and DC == 2
    NPAD = N + 9

    ctx = ExitStack()
    with ctx:
        def sb(name, shape, dt=F32):
            return ctx.enter_context(nc.sbuf_tensor(name, shape, dt))

        x1_d = nc.dram_tensor("x1_d", [NP, D], F32).ap()
        x2_d = nc.dram_tensor("x2_d", [NP, D], F32).ap()
        x3_d = nc.dram_tensor("x3_d", [NP, D], F32).ap()
        z_d = nc.dram_tensor("z_d", [NP, D], F32).ap()
        v3_d = nc.dram_tensor("v3_d", [NT, P, D], F32).ap()
        qk_d = nc.dram_tensor("qk_d", [NT, P, P], F32).ap()
        tiled = lambda d: d.rearrange("(t p) c -> t p c", p=P)
        xin_t, x1_t, x2_t, x3_t, z_t = (tiled(d) for d in (xin, x1_d, x2_d, x3_d, z_d))

        ident = sb("ident", [P, P])
        ones = sb("ones", [P, 2])
        wd = sb("wd", [P, DC, D])
        wqk = sb("wqk", [P, DC, P])
        ua = sb("ua", [P, DC, 2 * D])
        ub = sb("ub", [P, DC, 2 * D])
        uc = sb("uc", [P, DC, 2 * D])
        bias0 = sb("bias0", [P, D])
        gam = sb("gam", [P, D])
        bet = sb("bet", [P, D])
        tb = sb("tb", [P, 1])
        omt = sb("omt", [P, 1])
        expo = sb("expo", [P, NT])
        ln_const = sb("ln_const", [P, 3])
        rs = sb("rs", [P, NT])
        cs = sb("cs", [P, NT])
        cpart = sb("cpart", [P, 2, NT])
        d0 = sb("d0", [P, NT])
        d1 = sb("d1", [P, NT])
        dinf = sb("dinf", [P, NT], I32)
        zero = sb("zero", [P, NT])
        ir = sb("ir", [P, NT])
        ic = sb("ic", [P, NT])
        adj = sb("adj", [P, 2, NT, P])
        a1t, a2 = adj[0:A, 0, 0:DC, :], adj[0:A, 1, 0, 0:A]
        big = sb("big", [P, NT, 2 * D])
        Ha = big[:, :, 0:D]
        Hb = big[:, :, D:2 * D]
        Hc = sb("Hc", [P, NT, D])
        qk = sb("qk", [P, NP])
        stat = sb("stat", [P, 2, 8])
        xt = sb("xt", [P, 2, D])
        xn = sb("xn", [P, 2, D])
        t0 = sb("t0", [P, 2, D])
        t1 = sb("t1", [P, 2, D])
        cc = sb("cc", [P, 2, D])
        junk = sb("junk", [P, D])
        hT = sb("hT", [P, DC, P])

        banks = [ctx.enter_context(nc.psum_tensor(f"bank{i}", [P, 512], F32)) for i in range(8)]
        lg, tr = banks[0:2], banks[2:4]
        agg, axp, misc, dense = banks[4:8]

        def ln_act(act, sems, idx, par, src, dst, func):
            ln_a, ln_p = sems
            nc.scalar.activation(junk[:], src, ACT.Copy, accum_out=stat[:, par, 0:1]).then_inc(ln_a, 1)
            act.wait_ge(ln_p, 5 * idx + 1)
            act.wait_ge(ln_a, 2 * idx + 1)
            nc.scalar.activation(junk[:], src, ACT.Square, bias=stat[:, par, 1:2],
                                 accum_out=stat[:, par, 2:3]).then_inc(ln_a, 1)
            act.wait_ge(ln_p, 5 * idx + 5)
            act.wait_ge(ln_a, 2 * idx + 2)
            return nc.scalar.activation(dst, src, func, bias=stat[:, par, 5:6], scale=stat[:, par, 4:5])

        def ln_pool(pool, sems, idx, par):
            ln_a, ln_p = sems
            pool.wait_ge(ln_a, 2 * idx + 1)
            nc.gpsimd.tensor_tensor(stat[:, par, 1:2], stat[:, par, 0:1], ln_const[:, 0:1], ALU.mult).then_inc(ln_p, 1)
            pool.wait_ge(ln_a, 2 * idx + 2)
            nc.gpsimd.tensor_tensor(stat[:, par, 3:4], stat[:, par, 2:3], ln_const[:, 1:2], ALU.mult).then_inc(ln_p, 1)
            pool.wait_ge(ln_p, 5 * idx + 2)
            nc.gpsimd.tensor_tensor(stat[:, par, 6:7], stat[:, par, 3:4], ln_const[:, 2:3], ALU.add).then_inc(ln_p, 1)
            pool.wait_ge(ln_p, 5 * idx + 3)
            nc.gpsimd.tensor_tensor(stat[:, par, 4:5], stat[:, par, 6:7], expo[:, 0:1], ALU.pow).then_inc(ln_p, 1)
            pool.wait_ge(ln_p, 5 * idx + 4)
            nc.gpsimd.tensor_tensor(stat[:, par, 5:6], stat[:, par, 1:2], stat[:, par, 4:5],
                                    ALU.mult).then_inc(ln_p, 1)

        with phase_semaphores(nc) as s:
            loaded, idz, made, w12, cdone = (s(n) for n in (
                "c_loaded", "c_ident_zero", "c_made", "c_w12", "c_copied"))
            with nc.Block() as block:
                @block.sync
                def _(sp):
                    chunked = lambda w: w.rearrange("(c p) f -> p c f", p=P)
                    loads = [(wqk[:, :, 0:A], chunked(A3)), (a1t, A1T.rearrange("a (c p) -> a c p", p=P)),
                             (a2, A2), (ua[:], chunked(UA)), (ub[:], chunked(UB)), (uc[:], chunked(UC)),
                             (bias0[:], b0.partition_broadcast(P)), (gam[:], gamma.partition_broadcast(P)),
                             (bet[:], beta.partition_broadcast(P)), (tb[:], tin.partition_broadcast(P))]
                    for dst, src in loads:
                        sp.dma_start(dst, src).then_inc(loaded, 16)
                    sp.wait_ge(loaded, 16 * len(loads))

                @block.gpsimd
                def _(pool):
                    nc.gpsimd.memset(ident[:], 0.0).then_inc(idz, 1)
                    nc.gpsimd.memset(ones[:], 1.0)
                    nc.gpsimd.memset(expo[:], -0.5)
                    for i, value in enumerate((-1.0 / D, 1.0 / D, LN_EPS)):
                        nc.gpsimd.memset(ln_const[:, i:i + 1], value)
                    nc.gpsimd.memset(zero[:], 0.0)
                    pool.wait_ge(idz, 1)
                    nc.gpsimd.affine_select(out=ident[:], in_=ident[:], compare_op=ALU.not_equal, fill=1.0, base=0,
                                            pattern=[[-1, P]], channel_multiplier=1).then_inc(made, 1)

                @block.tensor
                def _(pe):
                    pe.wait_ge(loaded, 16 * 10)
                    for c in range(DC):
                        last = nc.tensor.matmul(misc[:, c * A:(c + 1) * A], a1t[:, c, :], a2, start=True, stop=True)
                    last.then_inc(w12, 1)

                @block.vector
                def _(dve):
                    dve.wait_ge(w12, 1)
                    nc.vector.tensor_copy(wqk[:, :, A:2 * A],
                                          misc[:, 0:DC * A].rearrange("p (c a) -> p c a", c=DC)).then_inc(cdone, 1)
                    dve.wait_ge(loaded, 16 * 10)
                    nc.vector.tensor_scalar(omt[:], tb[:], -1.0, 1.0, ALU.mult, ALU.add).then_inc(cdone, 1)

                @block.scalar
                def _(act):
                    act.wait_ge(cdone, 2)

        def layer(name, src_t, rowsum=False, rhs=None, plus_self=True, evac=None, dst_t=None,
                  nxt=None, weight=None, hnext=None, colsum=False):
            two_stage = nxt is not None
            use_adj = rowsum or rhs is not None
            with phase_semaphores(nc, name + "_") as s:
                weight_in = s("weight_in")
                adj_in = [s("adj_in0"), s("adj_in1")]
                x_in = [s("x_in0"), s("x_in1")]
                x_out = [s("x_out0"), s("x_out1")]
                agg_done, agg_copied, summed = s("agg_done"), s("agg_copied"), s("col_summed")
                pre, xnew = s("pre_added"), s("x_new")
                normed, transposed, hT_ready, dense_done, dense_copied = (
                    s("normed"), s("transposed"), s("hT_ready"), s("dense_done"), s("dense_copied"))
                h_kept, rs_ready = s("h_kept"), s("rs_ready")
                ln = (s("ln_act"), s("ln_pool"))
                acc = banks[4:6]
                xsrc = xt if evac is None else xn

                with nc.Block() as block:
                    @block.sync
                    def _(sp):
                        def body(u, par, live):
                            if live[0] and use_adj:
                                if not isinstance(u, int) or u >= 2:
                                    sp.wait_ge(agg_done, u - 1)
                                    if colsum:
                                        sp.wait_ge(summed, u - 1)
                                sp.dma_start(adj[:, par], adjT[u]).then_inc(adj_in[par], 16)
                            if live[0]:
                                if not isinstance(u, int) or u >= 2:
                                    if evac is None:
                                        sp.wait_ge(normed, u - 1)
                                    else:
                                        sp.wait_ge(xnew, u - 1)
                                sp.dma_start(xt[:, par], src_t[u]).then_inc(x_in[par], 16)
                            if live[1] and evac is not None:
                                sp.wait_ge(xnew, u)
                                sp.dma_start(dst_t[u - 1], xn[:, 1 - par]).then_inc(x_out[1 - par], 16)
                        if weight is not None:
                            sp.dma_start(wd[:], weight.rearrange("(c p) f -> p c f", p=P)).then_inc(weight_in, 16)
                        pipeline(sp, NT, body)
                        if evac is not None:
                            for par in range(2):
                                sp.wait_ge(x_out[par], 16 * (NT // 2))

                    @block.tensor
                    def _(pe):
                        def body(u, par, live):
                            if live[2] and two_stage:
                                pe.wait_ge(normed, u - 1)
                                if not isinstance(u, int) or u >= 3:
                                    pe.wait_ge(hT_ready, u - 2)
                                for c in range(DC):
                                    last = nc.tensor.transpose(misc[:, c * P:(c + 1) * P], cc[:, par, c * P:(c + 1) * P],
                                                               ident[:])
                                last.then_inc(transposed, 1)
                            if live[0] and use_adj:
                                pe.wait_ge(adj_in[par], 8 * u + (16 if par == 0 else 8))
                                if not isinstance(u, int) or u >= 2:
                                    pe.wait_ge(agg_copied, u - 1)
                                if rowsum:
                                    for j in range(NT):
                                        last = nc.tensor.matmul(acc[par][:, 0:1], adj[:, par, j], ones[:, 0:1],
                                                                start=(j == 0), stop=(j == NT - 1))
                                else:
                                    for j in range(NT):
                                        last = nc.tensor.matmul(acc[par][:, 0:D], adj[:, par, j], rhs[:, j],
                                                                start=(j == 0), stop=(j == NT - 1 and not plus_self))
                                    if plus_self:
                                        last = nc.tensor.matmul(acc[par][:, 0:D], ident[:], rhs[:, u],
                                                                start=False, stop=True)
                                last.then_inc(agg_done, 1)
                            if live[2] and two_stage:
                                pe.wait_ge(hT_ready, u - 1)
                                if not isinstance(u, int) or u >= 3:
                                    pe.wait_ge(dense_copied, u - 2)
                                for c in range(DC):
                                    if nxt == "dense":
                                        last = nc.tensor.matmul(dense[:, 0:D], hT[:, c], wd[:, c],
                                                                start=(c == 0), stop=(c == DC - 1))
                                    else:
                                        last = nc.tensor.matmul(dense[:, 0:P], wqk[:, c], hT[:, c],
                                                                start=(c == 0), stop=(c == DC - 1))
                                last.then_inc(dense_done, 1)
                        if weight is not None:
                            pe.wait_ge(weight_in, 16)
                        pipeline(pe, NT, body)

                    @block.scalar
                    def _(act):
                        def body(u, par, live):
                            if live[2] and two_stage:
                                act.wait_ge(transposed, u - 1)
                                if not isinstance(u, int) or u >= 3:
                                    act.wait_ge(dense_done, u - 2)
                                nc.scalar.activation(hT[:].rearrange("p c i -> p (c i)"), misc[:, 0:D],
                                                     ACT.Copy).then_inc(hT_ready, 1)
                            if live[0] and evac is not None:
                                act.wait_ge(agg_done, u + 1)
                                if not isinstance(u, int) or u >= 2:
                                    act.wait_ge(xnew, u - 1)
                                if evac == "layer0":
                                    nc.scalar.activation(t0[:, par], acc[par][:, 0:D], ACT.Copy,
                                                         scale=d0[:, bass.ds(u, 1)]).then_inc(agg_copied, 1)
                                elif evac == "layer1":
                                    nc.scalar.activation(t0[:, par], acc[par][:, 0:D], ACT.Relu,
                                                         scale=d1[:, bass.ds(u, 1)]).then_inc(agg_copied, 1)
                                else:
                                    nc.scalar.activation(t1[:, par], rhs[:, u], ACT.Copy, scale=omt[:])
                                    nc.scalar.activation(t0[:, par], acc[par][:, 0:D], ACT.Copy,
                                                         scale=tb[:]).then_inc(agg_copied, 1)
                            if live[0] and two_stage:
                                if evac is None:
                                    act.wait_ge(x_in[par], 8 * u + (16 if par == 0 else 8))
                                else:
                                    act.wait_ge(xnew, u + 1)
                                if not isinstance(u, int) or u >= 2:
                                    act.wait_ge(transposed, u - 1)
                                    if nxt == "attention":
                                        act.wait_ge(h_kept, u - 1)
                                ln_act(act, ln, u, par, xsrc[:, par], cc[:, par], ACT.Relu).then_inc(normed, 1)
                        pipeline(act, NT, body)

                    @block.gpsimd
                    def _(pool):
                        def body(u, par, live):
                            if live[0] and evac is not None:
                                pool.wait_ge(x_in[par], 8 * u + (16 if par == 0 else 8))
                                if not isinstance(u, int) or u >= 2:
                                    pool.wait_ge(x_out[par], 8 * u + (0 if par == 0 else -8))
                                    if two_stage:
                                        pool.wait_ge(normed, u - 1)
                                if evac == "layer0":
                                    nc.gpsimd.tensor_tensor(xt[:, par], xt[:, par], bias0[:], ALU.add).then_inc(pre, 1)
                                    pool.wait_ge(pre, u + 1)
                                    pool.wait_ge(agg_copied, u + 1)
                                elif evac == "layer1":
                                    pool.wait_ge(agg_copied, u + 1)
                                else:
                                    pool.wait_ge(agg_copied, u + 1)
                                    nc.gpsimd.tensor_tensor(xt[:, par], xt[:, par], t1[:, par], ALU.add).then_inc(pre, 1)
                                    pool.wait_ge(pre, u + 1)
                                nc.gpsimd.tensor_tensor(xn[:, par], xt[:, par], t0[:, par], ALU.add).then_inc(xnew, 1)
                            if live[0] and two_stage:
                                ln_pool(pool, ln, u, par)
                            if live[0] and nxt == "attention":
                                pool.wait_ge(normed, u + 1)
                                nc.gpsimd.tensor_copy(Hc[:, u], cc[:, par]).then_inc(h_kept, 1)
                        pipeline(pool, NT, body)

                    @block.vector
                    def _(dve):
                        def body(u, par, live):
                            if live[0] and rowsum:
                                dve.wait_ge(agg_done, u + 1)
                                nc.vector.tensor_scalar(rs[:, bass.ds(u, 1)], acc[par][:, 0:1], 1.0, None,
                                                        ALU.add).then_inc(agg_copied, 1)
                            if live[0] and colsum:
                                dve.wait_ge(adj_in[par], 8 * u + (16 if par == 0 else 8))
                                if not isinstance(u, int) or u >= 2:
                                    dve.wait_ge(csadd, u - 1)
                                nc.vector.reduce_sum(cpart[:, par], adj[:, par], axis=AX_X).then_inc(summed, 1)
                                dve.wait_ge(summed, u + 1)
                                if not isinstance(u, int) or u >= 1:
                                    dve.wait_ge(csadd, u)
                                if isinstance(u, int) and u == 0:
                                    nc.vector.tensor_scalar(cs[:], cpart[:, par], 1.0, None, ALU.add).then_inc(csadd, 1)
                                else:
                                    nc.vector.tensor_tensor(cs[:], cs[:], cpart[:, par], ALU.add).then_inc(csadd, 1)
                            if live[2] and two_stage:
                                dve.wait_ge(dense_done, u - 1)
                                if nxt == "attention":
                                    nc.vector.tensor_copy(qk[:, bass.ds((u - 2) * P, P)],
                                                          dense[:, 0:P]).then_inc(dense_copied, 1)
                                elif evac is None:
                                    nc.vector.tensor_copy(hnext[:, u - 2], dense[:, 0:D]).then_inc(dense_copied, 1)
                                else:
                                    nc.vector.tensor_scalar(hnext[:, u - 2], dense[:, 0:D], d1[:, bass.ds(u - 2, 1)], None,
                                                            ALU.mult).then_inc(dense_copied, 1)
                        csadd = s("cs_added")
                        pipeline(dve, NT, body)
                        if colsum:
                            dve.wait_ge(csadd, NT)
                            nc.vector.tensor_scalar(cs[:], cs[:], CLIP, None, ALU.max).then_inc(csadd, 1)
                            dve.wait_ge(csadd, NT + 1)
                            nc.vector.reciprocal(ic[:], cs[:]).then_inc(csadd, 1)
                            dve.wait_ge(csadd, NT + 2)

        xz = sb("xz", [P, 2, D])

        layer("rowsum", xin_t, rowsum=True, nxt="dense", weight=W0T, hnext=Ha)

        with phase_semaphores(nc) as s:
            powd, fin = s("n_pow"), s("n_fin")
            with nc.Block() as block:
                @block.gpsimd
                def _(pool):
                    nc.gpsimd.tensor_tensor(d0[:], rs[:], expo[:], ALU.pow).then_inc(powd, 1)

                @block.vector
                def _(dve):
                    nc.vector.tensor_scalar(dinf[:], rs[:], 0.0, None, ALU.is_equal).then_inc(fin, 1)
                    nc.vector.tensor_scalar(ir[:], rs[:], CLIP, None, ALU.max).then_inc(fin, 1)
                    dve.wait_ge(powd, 1)
                    nc.vector.tensor_copy(d1[:], d0[:]).then_inc(fin, 1)
                    dve.wait_ge(fin, 3)
                    nc.vector.copy_predicated(d1[:], dinf[:], zero[:]).then_inc(fin, 1)
                    nc.vector.reciprocal(ir[:], ir[:]).then_inc(fin, 1)
                    for j in range(NT):
                        nc.vector.tensor_scalar(Ha[:, j], Ha[:, j], d0[:, j:j + 1], None, ALU.mult).then_inc(fin, 1)
                    dve.wait_ge(fin, 5 + NT)

        layer("layer0", xin_t, rhs=Ha, evac="layer0", dst_t=x1_t, nxt="dense", weight=W1g, hnext=Hb, colsum=True)
        layer("layer1", x1_t, rhs=Hb, evac="layer1", dst_t=x2_t, nxt="attention")

        with ExitStack() as att:
            ab = lambda name, shape, dt=F32: att.enter_context(nc.sbuf_tensor(name, shape, dt))
            E = ab("E", [P, 2, NP])
            U = ab("U", [P, NPAD])
            PT = ab("PT", [P, NT, P])
            qt = ab("qt", [A, 2, P])
            g = bias0
            gT, xaT = (wd[:, i].rearrange("p (c i) -> p c i", c=DC) for i in range(2))
            gTf, xaTf = wd[:, 0], wd[:, 1]
            qkb = hT
            zo = ab("zo", [P, 2, D])
            nmax = ab("nmax", [P, 2])
            Zs = ab("Zs", [P, 2])
            rz = ab("rz", [P, 2])
            tgt = ab("tgt", [P, 1])
            lo = ab("lo", [P, 3])
            hi = ab("hi", [P, 3])
            new = ab("new", [P, 3])
            up = ab("up", [P, 3], I32)
            down = ab("down", [P, 3], I32)
            sc = ab("sc", [P, 8])
            keep = ab("keep", [P, TOP], I32)
            top8 = ab("top8", [P, TOP])
            mark = ab("mark", [P, TOP])
            mass = ab("mass", [P, TOP + 1])
            kmass = ab("kmass", [P, TOP])
            ones8 = ab("ones8", [P, TOP])
            flag = ab("flag", [P, 32])
            flagT = ab("flagT", [P, 32])
            flagm = ab("flagm", [P, 1])
            flagi = ab("flagi", [P, 1], I32)

            for step in range(2):
                with phase_semaphores(nc, f"att{step}_") as s:
                    adj_in = [s("adj_in0"), s("adj_in1")]
                    ops_in = s("operands_in")
                    x_in = [s("x_in0"), s("x_in1")]
                    z_out = [s("z_out0"), s("z_out1")]
                    q_ready, lg_done, lg_copied = s("q_ready"), s("lg_done"), s("lg_copied")
                    tr_done, pt_copied = s("tr_done"), s("pt_copied")
                    max_ready, exp_done, probs_ready = s("max_ready"), s("exp_done"), s("probs_ready")
                    agg_done, agg_copied, ax_done, ax_copied = (
                        s("agg_done"), s("agg_copied"), s("ax_done"), s("ax_copied"))
                    g_ready, gT_done, gT_ready = s("g_ready"), s("gT_done"), s("gT_ready")
                    xa_ready, xT_done, xT_ready = s("xa_ready"), s("xT_done"), s("xT_ready")
                    ua_done, ua_copied, ub_done = s("ua_done"), s("ua_copied"), s("ub_done")
                    uc_done, qk_done, qk_copied = s("uc_done"), s("qk_done"), s("qk_copied")
                    z_part, z_mid, z_done = s("z_part"), s("z_mid"), s("z_done")
                    ln = (s("ln_act"), s("ln_pool"))
                    y_ready, c_ready, x_pre = s("y_ready"), s("c_ready"), s("x_pre")
                    search, rnd = s("search_step"), s("round_step")
                    V = big
                    later = lambda u, k: not isinstance(u, int) or u >= k
                    slot = lambda t, par: 8 * t + (16 if par == 0 else 8)

                    with nc.Block() as block:
                        @block.sync
                        def _(sp):
                            if step == 1:
                                sp.dma_start(qk[:].rearrange("p (t i) -> p t i", i=P),
                                             qk_d.rearrange("t p i -> p t i")).then_inc(ops_in, 16)
                                sp.dma_start(Hc[:], v3_d.rearrange("t p c -> p t c")).then_inc(ops_in, 16)

                            def body(u, par, live):
                                if live[0]:
                                    if later(u, 2):
                                        sp.wait_ge(agg_done, u - 1)
                                    sp.dma_start(adj[:, par], adjT[u]).then_inc(adj_in[par], 16)
                                if step == 0 and live[2]:
                                    sp.wait_ge(z_done, u - 1)
                                    sp.dma_start(z_t[u - 2], zo[:, par]).then_inc(z_out[par], 16)
                                    sp.wait_ge(ax_copied, u - 1)
                                    sp.dma_start(v3_d[u - 2], xn[:, par]).then_inc(z_out[par], 16)
                                    sp.wait_ge(qk_copied, u - 1)
                                    sp.dma_start(qk_d[u - 2], qkb[:, par]).then_inc(z_out[par], 16)
                                if step == 1 and live[1]:
                                    if later(u, 3):
                                        sp.wait_ge(z_done, u - 2)
                                    sp.dma_start(xt[:, 1 - par], z_t[u - 1]).then_inc(x_in[1 - par], 16)
                                    sp.dma_start(xn[:, 1 - par], x2_t[u - 1]).then_inc(x_in[1 - par], 16)
                                if step == 1 and live[2]:
                                    sp.wait_ge(z_done, u - 1)
                                    sp.dma_start(x3_t[u - 2], zo[:, par]).then_inc(z_out[par], 16)
                            pipeline(sp, NT, body)
                            for par in range(2):
                                sp.wait_ge(z_out[par], 16 * (3 if step == 0 else 1) * (NT // 2))

                        @block.tensor
                        def _(pe):
                            if step == 1:
                                pe.wait_ge(ops_in, 32)

                            def body(u, par, live):
                                for k, (c0, cw) in enumerate(CHUNKS):
                                    ring = (par * KC + k) % 2
                                    if live[2]:
                                        if k == 0:
                                            pe.wait_ge(probs_ready, u - 1)
                                        if later(u, 3) or k >= 2:
                                            pe.wait_ge(pt_copied, KC * (u - 2) + k - 1)
                                        for i in range(cw // P):
                                            last = nc.tensor.transpose(tr[ring][:, i * P:(i + 1) * P],
                                                                       E[:, par, c0 + i * P:c0 + (i + 1) * P], ident[:])
                                        last.then_inc(tr_done, 1)
                                    if live[0]:
                                        if k == 0:
                                            pe.wait_ge(q_ready, u + 1)
                                        if later(u, 1) or k >= 2:
                                            pe.wait_ge(lg_copied, KC * u + k - 1)
                                        nc.tensor.matmul(lg[ring][:, 0:cw], qt[:, par], qk[0:A, c0:c0 + cw],
                                                         start=True, stop=True).then_inc(lg_done, 1)
                                if live[1]:
                                    q = 1 - par
                                    pe.wait_ge(adj_in[q], slot(u - 1, q))
                                    if later(u, 2):
                                        pe.wait_ge(agg_copied, u - 1)
                                    rhs = Hc if step == 0 else V
                                    w = D if step == 0 else 2 * D
                                    for j in range(NT):
                                        nc.tensor.matmul(agg[:, 0:w], adj[:, q, j], rhs[:, j], start=(j == 0), stop=False)
                                    nc.tensor.matmul(agg[:, 0:w], ident[:], rhs[:, u - 1],
                                                     start=False, stop=True).then_inc(agg_done, 1)
                                if live[2]:
                                    if later(u, 3):
                                        pe.wait_ge(ax_copied, u - 2)
                                    for k, (c0, cw) in enumerate(CHUNKS):
                                        pe.wait_ge(pt_copied, KC * (u - 2) + k + 1)
                                        for j in range(c0 // P, (c0 + cw) // P):
                                            last = nc.tensor.matmul(axp[:, 0:D], PT[:, j], Hc[:, j],
                                                                    start=(j == 0), stop=(j == NT - 1))
                                    last.then_inc(ax_done, 1)
                                if step == 1:
                                    return
                                if live[1]:
                                    pe.wait_ge(g_ready, u)
                                    if later(u, 3):
                                        pe.wait_ge(qk_copied, u - 2)
                                    for c in range(DC):
                                        last = nc.tensor.transpose(misc[:, c * P:(c + 1) * P], g[:, c * P:(c + 1) * P],
                                                                   ident[:])
                                    last.then_inc(gT_done, 1)
                                if live[2]:
                                    pe.wait_ge(xa_ready, u - 1)
                                    pe.wait_ge(ua_copied, u - 1)
                                    for c in range(DC):
                                        last = nc.tensor.transpose(dense[:, c * P:(c + 1) * P],
                                                                   cc[:, par, c * P:(c + 1) * P], ident[:])
                                    last.then_inc(xT_done, 1)
                                if live[1]:
                                    pe.wait_ge(gT_ready, u)
                                    if live[2]:
                                        pe.wait_ge(xT_ready, u - 1)
                                    for bank, wt, done in ((dense, ua, ua_done), (agg, ub, ub_done)):
                                        for c in range(DC):
                                            last = nc.tensor.matmul(bank[:, 0:2 * D], gT[:, c], wt[:, c],
                                                                    start=(c == 0), stop=(c == DC - 1))
                                        last.then_inc(done, 1)
                                if live[2]:
                                    pe.wait_ge(xT_ready, u - 1)
                                    for c in range(DC):
                                        last = nc.tensor.matmul(axp[:, 0:2 * D], xaT[:, c], uc[:, c],
                                                                start=(c == 0), stop=(c == DC - 1))
                                    last.then_inc(uc_done, 1)
                                    for c in range(DC):
                                        last = nc.tensor.matmul(misc[:, 0:P], wqk[:, c], xaT[:, c],
                                                                start=(c == 0), stop=(c == DC - 1))
                                    last.then_inc(qk_done, 1)
                            pipeline(pe, NT, body)

                        @block.scalar
                        def _(act):
                            if step == 1:
                                act.wait_ge(ops_in, 32)

                            def body(u, par, live):
                                q = 1 - par
                                if live[0]:
                                    if later(u, 2):
                                        act.wait_ge(lg_done, KC * (u - 1))
                                    nc.scalar.activation(qt[:, par], qk[A:2 * A, bass.ds(u * P, P)],
                                                         ACT.Copy).then_inc(q_ready, 1)
                                for k, (c0, cw) in enumerate(CHUNKS):
                                    ring = (par * KC + k) % 2
                                    if live[2]:
                                        act.wait_ge(tr_done, KC * (u - 2) + k + 1)
                                        if k == 0 and later(u, 3):
                                            act.wait_ge(ax_done, u - 2)
                                        nc.scalar.activation(PT[:].rearrange("p t i -> p (t i)")[:, c0:c0 + cw],
                                                             tr[ring][:, 0:cw], ACT.Copy).then_inc(pt_copied, 1)
                                    if live[0]:
                                        act.wait_ge(lg_done, KC * u + k + 1)
                                        nc.scalar.activation(E[:, par, c0:c0 + cw], lg[ring][:, 0:cw],
                                                             ACT.Copy).then_inc(lg_copied, 1)
                                if live[0]:
                                    act.wait_ge(max_ready, u + 1)
                                    act.wait_ge(lg_copied, KC * (u + 1))
                                    nc.scalar.activation(E[:, par, 0:N], E[:, par, 0:N], ACT.Exp, bias=nmax[:, par:par + 1],
                                                         accum_out=Zs[:, par:par + 1]).then_inc(exp_done, 1)
                                if step == 0:
                                    if live[1]:
                                        act.wait_ge(agg_done, u)
                                        nc.scalar.activation(g[:], agg[:, 0:D], ACT.Copy).then_inc(g_ready, 1)
                                    if live[2]:
                                        act.wait_ge(ax_done, u - 1)
                                        nc.scalar.activation(cc[:, par], axp[:, 0:D], ACT.Copy,
                                                             scale=rz[:, par:par + 1]).then_inc(xa_ready, 1)
                                    if live[1]:
                                        act.wait_ge(gT_done, u)
                                        nc.scalar.activation(gTf, misc[:, 0:D],
                                                             ACT.Copy).then_inc(gT_ready, 1)
                                    if live[2]:
                                        act.wait_ge(xT_done, u - 1)
                                        nc.scalar.activation(xaTf, dense[:, 0:D],
                                                             ACT.Copy).then_inc(xT_ready, 1)
                                    if live[1]:
                                        act.wait_ge(ua_done, u)
                                        if later(u, 3):
                                            act.wait_ge(z_part, u - 2)
                                        nc.scalar.activation(t0[:, q], dense[:, 0:D], ACT.Copy, scale=ir[:, bass.ds(u - 1, 1)])
                                        nc.scalar.activation(t1[:, q], dense[:, D:2 * D], ACT.Copy,
                                                             scale=ic[:, bass.ds(u - 1, 1)]).then_inc(ua_copied, 1)
                                        act.wait_ge(ub_done, u)
                                        nc.scalar.activation(V[:, u - 1, 0:D], agg[:, 0:D], ACT.Copy,
                                                             scale=ir[:, bass.ds(u - 1, 1)])
                                        nc.scalar.activation(V[:, u - 1, D:2 * D], agg[:, D:2 * D], ACT.Copy,
                                                             scale=ic[:, bass.ds(u - 1, 1)]).then_inc(agg_copied, 1)
                                    if live[2]:
                                        act.wait_ge(uc_done, u - 1)
                                        if later(u, 4):
                                            act.wait_ge(z_out[par], 24 * (u - 2) + (0 if par == 0 else -24))
                                            act.wait_ge(z_done, u - 3)
                                        nc.scalar.activation(xt[:, par], axp[:, 0:D], ACT.Copy)
                                        nc.scalar.activation(xn[:, par], axp[:, D:2 * D], ACT.Copy).then_inc(ax_copied, 1)
                                        act.wait_ge(qk_done, u - 1)
                                        nc.scalar.activation(qkb[:, par], misc[:, 0:P], ACT.Copy).then_inc(qk_copied, 1)
                                else:
                                    if live[1]:
                                        act.wait_ge(agg_done, u)
                                        if later(u, 3):
                                            act.wait_ge(z_part, u - 2)
                                        nc.scalar.activation(t0[:, q], agg[:, 0:D], ACT.Copy, scale=ir[:, bass.ds(u - 1, 1)])
                                        nc.scalar.activation(t1[:, q], agg[:, D:2 * D], ACT.Copy,
                                                             scale=ic[:, bass.ds(u - 1, 1)]).then_inc(agg_copied, 1)
                                    if live[2]:
                                        act.wait_ge(ax_done, u - 1)
                                        if later(u, 3):
                                            act.wait_ge(y_ready, u - 2)
                                        nc.scalar.activation(g[:], axp[:, 0:D], ACT.Copy,
                                                             scale=rz[:, par:par + 1]).then_inc(ax_copied, 1)
                                        act.wait_ge(y_ready, u - 1)
                                        if later(u, 4):
                                            act.wait_ge(z_done, u - 3)
                                        ln_act(act, ln, u - 2, par, xt[:, par], cc[:, par], ACT.Identity).then_inc(c_ready, 1)
                            pipeline(act, NT, body)

                        @block.gpsimd
                        def _(pool):
                            def body(u, par, live):
                                q = 1 - par
                                if step == 0:
                                    if live[1]:
                                        pool.wait_ge(ua_copied, u)
                                        nc.gpsimd.tensor_tensor(t0[:, q], t0[:, q], t1[:, q], ALU.add).then_inc(z_mid, 1)
                                        pool.wait_ge(z_mid, u)
                                        if later(u, 3):
                                            pool.wait_ge(z_done, u - 2)
                                        nc.gpsimd.tensor_tensor(xz[:, q], t0[:, q], Hc[:, u - 1], ALU.add).then_inc(z_part, 1)
                                    if live[2]:
                                        pool.wait_ge(ax_copied, u - 1)
                                        pool.wait_ge(z_part, u - 1)
                                        if later(u, 4):
                                            pool.wait_ge(z_out[par], 24 * (u - 2) + (0 if par == 0 else -24))
                                        nc.gpsimd.tensor_tensor(zo[:, par], xz[:, par], xt[:, par], ALU.add).then_inc(z_done, 1)
                                else:
                                    if live[1]:
                                        pool.wait_ge(agg_copied, u)
                                        nc.gpsimd.tensor_tensor(t0[:, q], t0[:, q], t1[:, q], ALU.add).then_inc(z_mid, 1)
                                        pool.wait_ge(z_mid, u)
                                        pool.wait_ge(x_in[q], 2 * slot(u - 1, q))
                                        nc.gpsimd.tensor_tensor(xt[:, q], xt[:, q], t0[:, q], ALU.add).then_inc(z_part, 1)
                                    if live[2]:
                                        pool.wait_ge(ax_copied, u - 1)
                                        pool.wait_ge(z_part, u - 1)
                                        nc.gpsimd.tensor_tensor(xt[:, par], xt[:, par], g[:], ALU.add).then_inc(y_ready, 1)
                                        nc.gpsimd.tensor_tensor(xn[:, par], xn[:, par], bet[:], ALU.add).then_inc(x_pre, 1)
                                        ln_pool(pool, ln, u - 2, par)
                                        pool.wait_ge(c_ready, u - 1)
                                        nc.gpsimd.tensor_tensor(cc[:, par], cc[:, par], gam[:], ALU.mult).then_inc(x_pre, 1)
                                        pool.wait_ge(x_pre, 2 * (u - 1))
                                        if later(u, 4):
                                            pool.wait_ge(z_out[par], 8 * (u - 2) + (0 if par == 0 else -8))
                                        nc.gpsimd.tensor_tensor(zo[:, par], xn[:, par], cc[:, par],
                                                                ALU.add).then_inc(z_done, 1)
                            pipeline(pool, NT, body)

                        @block.vector
                        def _(dve):
                            V_ = nc.vector
                            more = dve.alloc_register(f"rounds_end{step}")
                            open_rows = [dve.alloc_register(f"open{step}_{i}") for i in range(4)]
                            V_.memset(ones8[:], 1.0).then_inc(search, 1)
                            V_.memset(flag[:], 0.0).then_inc(search, 1)
                            dve.wait_ge(search, 2)

                            def body(u, par, live):
                                q = 1 - par
                                count = [0]

                                def then(*ins):
                                    for i in ins:
                                        i.then_inc(search, 1)
                                    count[0] += len(ins)
                                    dve.wait_ge(search, count[0])

                                dve.sem_clear(search)

                                def row_max():
                                    dve.wait_ge(lg_copied, KC * (u + 1))
                                    if later(u, 2):
                                        dve.wait_ge(exp_done, u - 1)
                                    V_.tensor_reduce(nmax[:, par:par + 1], E[:, par, 0:N], axis=AX_X, op=ALU.max,
                                                     negate=True).then_inc(max_ready, 1)
                                if not live[1]:
                                    if live[0]:
                                        row_max()
                                    return
                                e = E[:, q, 0:N]
                                dve.wait_ge(exp_done, u)
                                then(V_.tensor_scalar(tgt[:], Zs[:, q:q + 1], P_NUC, None, ALU.mult),
                                     V_.tensor_scalar(lo[:, 1:2], Zs[:, q:q + 1], 1 - P_NUC, None, ALU.mult),
                                     V_.tensor_scalar(hi[:, 1:2], Zs[:, q:q + 1], -P_NUC, None, ALU.mult),
                                     V_.memset(lo[:, 0:1], 0.0), V_.memset(hi[:, 0:1], 1.5),
                                     V_.memset(lo[:, 2:3], 0.0), V_.memset(hi[:, 2:3], 0.0),
                                     V_.memset(new[:, 0:1], FIRST_GUESS))
                                for k in range(EVALS[step]):
                                    then(V_.tensor_scalar(sc[:, 0:1], new[:, 0:1], AIM, tgt[:], ALU.mult, ALU.subtract),
                                         V_.tensor_scalar(lo[:, 1:2], lo[:, 1:2], KEEP_END, None, ALU.mult),
                                         V_.tensor_scalar(hi[:, 1:2], hi[:, 1:2], KEEP_END, None, ALU.mult),
                                         V_.scalar_tensor_tensor(out=U[:, 0:N], in0=e, scalar=new[:, 0:1], in1=e,
                                                                 op0=ALU.is_ge, op1=ALU.mult, accum_out=new[:, 2:3]))
                                    then(V_.tensor_tensor(new[:, 1:2], new[:, 2:3], sc[:, 0:1], ALU.add),
                                         V_.tensor_scalar(up[:], new[:, 2:3].to_broadcast([P, 3]), tgt[:], None, ALU.is_ge),
                                         V_.tensor_scalar(down[:], new[:, 2:3].to_broadcast([P, 3]), tgt[:], None, ALU.is_lt))
                                    then(V_.copy_predicated(lo[:], up[:], new[:]), V_.copy_predicated(hi[:], down[:], new[:]))
                                    if k < EVALS[step] - 1:
                                        then(V_.tensor_tensor(sc[:, 1:2], lo[:, 1:2], hi[:, 1:2], ALU.subtract),
                                             V_.tensor_tensor(sc[:, 2:3], hi[:, 0:1], lo[:, 0:1], ALU.subtract))
                                        then(V_.reciprocal(sc[:, 3:4], sc[:, 1:2]),
                                             V_.tensor_tensor(sc[:, 4:5], sc[:, 2:3], lo[:, 1:2], ALU.mult))
                                        then(V_.scalar_tensor_tensor(out=sc[:, 5:6], in0=sc[:, 4:5], scalar=sc[:, 3:4],
                                                                     in1=lo[:, 0:1], op0=ALU.mult, op1=ALU.add))
                                        then(V_.tensor_tensor(new[:, 0:1], sc[:, 5:6], hi[:, 0:1], ALU.min))
                                    if k == 2 and live[0]:
                                        row_max()
                                then(V_.scalar_tensor_tensor(out=U[:, 0:N], in0=e, scalar=hi[:, 0:1], in1=e,
                                                             op0=ALU.is_ge, op1=ALU.subtract, reverse1=True),
                                     V_.tensor_copy(mass[:, 0:1], hi[:, 2:3]))
                                dve.reg_mov(more, 1)
                                with dve.Fori(0, more):
                                    dve.sem_clear(rnd)
                                    m = [0]

                                    def rthen(*ins):
                                        for i in ins:
                                            i.then_inc(rnd, 1)
                                        m[0] += len(ins)
                                        dve.wait_ge(rnd, m[0])
                                    rthen(V_.memset(U[:, N:NPAD], MARK_PAD), V_.memset(mark[:], MARK_PAD),
                                          V_.max(top8[:], U[:, 0:N]))
                                    rthen(V_.tensor_tensor_scan(mass[:, 1:TOP + 1], ones8[:], top8[:], mass[:, 0:1],
                                                                ALU.mult, ALU.add))
                                    rthen(V_.tensor_scalar(keep[:], mass[:, 0:TOP], tgt[:], None, ALU.is_lt),
                                          V_.scalar_tensor_tensor(out=kmass[:], in0=mass[:, 0:TOP], scalar=tgt[:],
                                                                  in1=mass[:, 1:TOP + 1], op0=ALU.is_lt, op1=ALU.mult))
                                    rthen(V_.copy_predicated(mark[:], keep[:], top8[:]),
                                          V_.reduce_max(sc[:, 6:7], kmass[:], axis=AX_X))
                                    rthen(V_.match_replace(U[:], mark[:], U[:], MARKED),
                                          V_.tensor_tensor(mass[:, 0:1], mass[:, 0:1], sc[:, 6:7], ALU.max))
                                    rthen(V_.tensor_scalar(flag[:, 0:1], mass[:, 0:1], tgt[:], None, ALU.is_lt))
                                    rthen(V_.transpose(flagT[:], flag[:]))
                                    rthen(V_.reduce_max(flagm[:], flagT[:], axis=AX_X))
                                    rthen(V_.tensor_copy(flagi[:], flagm[:]))
                                    for i in range(4):
                                        dve.reg_load(open_rows[i], flagi[32 * i:32 * i + 1, 0:1])
                                    dve.reg_add(open_rows[0], open_rows[0], open_rows[1])
                                    dve.reg_add(open_rows[2], open_rows[2], open_rows[3])
                                    dve.reg_add(open_rows[0], open_rows[0], open_rows[2])
                                    dve.reg_alu(open_rows[0], open_rows[0], NP, ALU.mult)
                                    dve.reg_mov(more, open_rows[0])
                                if later(u, 3):
                                    dve.wait_ge(xa_ready if step == 0 else ax_copied, u - 2)
                                V_.reciprocal(rz[:, q:q + 1], mass[:, 0:1]).then_inc(search, 1)
                                V_.scalar_tensor_tensor(out=e, in0=U[:, 0:N], scalar=0.0, in1=e,
                                                        op0=ALU.is_le, op1=ALU.mult).then_inc(search, 1)
                                V_.memset(E[:, q, N:NP], 0.0).then_inc(search, 1)
                                dve.wait_ge(search, count[0] + 3)
                                dve.sem_inc(probs_ready, 1)
                            pipeline(dve, NT, body)

        layer("operand3", x3_t, nxt="dense", weight=Wg3, hnext=Ha)
        layer("layer3", x3_t, rhs=Ha, plus_self=False, evac="layer3",
              dst_t=out.rearrange("(t p) c -> t p c", p=P))


def kernel(**inputs):
    from concourse import bacc
    from concourse.bass_utils import run_bass_kernel_spmd

    x = np.asarray(inputs["x"])
    adj = np.asarray(inputs["adj"])
    n, d = x.shape
    nt = -(-n // P)
    nt += nt % 2
    n_pad = nt * P
    xp = np.zeros((n_pad, d), np.float32)
    xp[:n] = x
    ap = np.zeros((n_pad, n_pad), np.float32)
    ap[:n, :n] = adj
    adjT = np.ascontiguousarray(ap.reshape(nt, P, nt, P).transpose(0, 3, 2, 1))
    w = {k: np.asarray(v) for k, v in inputs.items()}
    side = lambda a, b: np.ascontiguousarray(np.concatenate([a, b], axis=1))
    U1, U2, U3 = w["L2_gnn_U1"], w["L2_gnn_U2"], w["L2_gnn_U3"]
    arrays = {
        "xin": xp, "adjT": adjT, "W0T": np.ascontiguousarray(w["L0_gnn_W"].T), "b0": w["L0_gnn_b"],
        "W1g": w["L1_gnn_weight"], "A1T": np.ascontiguousarray(w["L2_gnn_W1"].T), "A2": w["L2_gnn_W2"],
        "A3": w["L2_gnn_W3"], "UA": side(U1[0], U2[0]), "UB": side(U1[1], U2[1]), "UC": side(U3[0], U3[1]),
        "gamma": w["L2_gnn_gamma"], "beta": w["L2_gnn_beta"], "tin": w["L3_gnn_t"], "Wg3": w["L3_gnn_weight"],
    }
    nc = bacc.Bacc("TRN2", target_bir_lowering=False, num_devices=1)
    args = {k: nc.dram_tensor(k, a.shape, mybir.dt.from_np(a.dtype), kind="ExternalInput").ap()
            for k, a in arrays.items()}
    out = nc.dram_tensor("out", (n_pad, d), F32, kind="ExternalOutput").ap()
    build(nc, n, out=out, **args)
    r = run_bass_kernel_spmd(nc, [arrays], core_ids=[0])
    return r.results[0]["out"][:n]
```

```python
from contextlib import ExitStack, contextmanager

import numpy as np
import concourse.bass as bass
from concourse import mybir

F32 = mybir.dt.float32
I32 = mybir.dt.int32
ALU = mybir.AluOpType
ACT = mybir.ActivationFunctionType
AX_X = mybir.AxisListType.X

P = 128
LN_EPS = 1e-5
CLIP = 1e-12
P_NUC = 0.9
TOP = 8
EVALS = (3, 5)
MAX_AFTER = (1, 2)
AIM = 3.0
KEEP_END = 0.8
FIXED = ((0.008, 0.03, 0.1), (0.008, 0.03, 0.1))
MARK_PAD = 5.0
MARKED = -1.0


@contextmanager
def phase_semaphores(nc, prefix=""):
    mine = []

    def new(name):
        mine.append(nc.alloc_semaphore(prefix + name))
        return mine[-1]
    yield new
    nc.clear_and_free_semaphores(mine)
    nc.all_engine_barrier()


def pipeline(eng, tiles, body, depth=2, lead=4):
    def static(u):
        body(u, u % 2, [0 <= u - k < tiles for k in range(depth + 1)])
    for u in range(lead):
        static(u)
    if tiles > lead:
        with eng.Fori(lead, tiles - 1, 2) as u:
            body(u, 0, [True] * (depth + 1))
            body(u + 1, 1, [True] * (depth + 1))
    for u in range(tiles, tiles + depth):
        static(u)


def between_floats(value):
    t = np.float32(3 * value)
    while True:
        t = np.nextafter(t, np.float32(np.inf))
        near = [np.float32(t / np.float32(3))]
        for _ in range(2):
            near = [np.nextafter(near[0], np.float32(0))] + near + [np.nextafter(near[-1], np.float32(np.inf))]
        if all(np.float32(3) * e != t and 3 * float(e) != float(t) for e in near):
            return float(min(e for e in near if 3 * float(e) > float(t))), float(t)


def build(nc, n_nodes, xin, adjR, adjT, W0T, b0, W1g, A1T, A2, A3, UA, UB, UC, gamma, beta, tin, Wg3, out):
    N = n_nodes
    NT = xin.shape[0] // P
    NP = NT * P
    D = xin.shape[1]
    DC = D // P
    A = A2.shape[0]
    CW = 512
    CHUNKS = [(c, min(CW, NP - c)) for c in range(0, NP, CW)]
    KC = len(CHUNKS)
    assert NT % 2 == 0 and DC == 2
    NPAD = N + 9

    ctx = ExitStack()
    with ctx:
        def sb(name, shape, dt=F32):
            return ctx.enter_context(nc.sbuf_tensor(name, shape, dt))

        x1_d = nc.dram_tensor("x1_d", [NP, D], F32).ap()
        x2_d = nc.dram_tensor("x2_d", [NP, D], F32).ap()
        x3_d = nc.dram_tensor("x3_d", [NP, D], F32).ap()
        z_d = nc.dram_tensor("z_d", [NP, D], F32).ap()
        v3_d = nc.dram_tensor("v3_d", [NT, P, D], F32).ap()
        qk_d = nc.dram_tensor("qk_d", [NT, P, P], F32).ap()
        tiled = lambda d: d.rearrange("(t p) c -> t p c", p=P)
        xin_t, x1_t, x2_t, x3_t, z_t = (tiled(d) for d in (xin, x1_d, x2_d, x3_d, z_d))

        ident = sb("ident", [P, P])
        ones = sb("ones", [P, 2])
        wd = sb("wd", [P, DC, D])
        wqk = sb("wqk", [P, DC, P])
        ua = sb("ua", [P, DC, 2 * D])
        ub = sb("ub", [P, DC, 2 * D])
        uc = sb("uc", [P, DC, 2 * D])
        bias0 = sb("bias0", [P, D])
        gam = sb("gam", [P, D])
        bet = sb("bet", [P, D])
        tb = sb("tb", [P, 1])
        omt = sb("omt", [P, 1])
        expo = sb("expo", [P, NT])
        ln_const = sb("ln_const", [P, 3])
        rs = sb("rs", [P, NT])
        cs = sb("cs", [P, NT])
        cpart = sb("cpart", [P, 2, NT])
        d0 = sb("d0", [P, NT])
        d1 = sb("d1", [P, NT])
        dinf = sb("dinf", [P, NT], I32)
        zero = sb("zero", [P, NT])
        ir = sb("ir", [P, NT])
        ic = sb("ic", [P, NT])
        adj = sb("adj", [P, 2, NT, P])
        a1t, a2 = adj[0:A, 0, 0:DC, :], adj[0:A, 1, 0, 0:A]
        big = sb("big", [P, NT, 2 * D])
        Ha = big[:, :, 0:D]
        Hb = big[:, :, D:2 * D]
        Hc = sb("Hc", [P, NT, D])
        qk = sb("qk", [P, NP])
        stat = sb("stat", [P, 2, 8])
        xt = sb("xt", [P, 2, D])
        xn = sb("xn", [P, 2, D])
        t0 = sb("t0", [P, 2, D])
        t1 = sb("t1", [P, 2, D])
        cc = sb("cc", [P, 2, D])
        junk = sb("junk", [P, NP], mybir.dt.uint8)
        hT = sb("hT", [P, DC, P])

        banks = [ctx.enter_context(nc.psum_tensor(f"bank{i}", [P, 512], F32)) for i in range(8)]
        lg, tr = banks[0:2], banks[2:4]
        agg, axp, misc, dense = banks[4:8]

        def ln_act(act, sems, idx, par, src, dst, func):
            ln_a, ln_p = sems
            nc.scalar.activation(junk[:, 0:D], src, ACT.Copy, accum_out=stat[:, par, 0:1]).then_inc(ln_a, 1)
            act.wait_ge(ln_p, 5 * idx + 1)
            act.wait_ge(ln_a, 2 * idx + 1)
            nc.scalar.activation(junk[:, 0:D], src, ACT.Square, bias=stat[:, par, 1:2],
                                 accum_out=stat[:, par, 2:3]).then_inc(ln_a, 1)
            act.wait_ge(ln_p, 5 * idx + 5)
            act.wait_ge(ln_a, 2 * idx + 2)
            return nc.scalar.activation(dst, src, func, bias=stat[:, par, 5:6], scale=stat[:, par, 4:5])

        def ln_pool(pool, sems, idx, par):
            ln_a, ln_p = sems
            pool.wait_ge(ln_a, 2 * idx + 1)
            nc.gpsimd.tensor_tensor(stat[:, par, 1:2], stat[:, par, 0:1], ln_const[:, 0:1], ALU.mult).then_inc(ln_p, 1)
            pool.wait_ge(ln_a, 2 * idx + 2)
            nc.gpsimd.tensor_tensor(stat[:, par, 3:4], stat[:, par, 2:3], ln_const[:, 1:2], ALU.mult).then_inc(ln_p, 1)
            pool.wait_ge(ln_p, 5 * idx + 2)
            nc.gpsimd.tensor_tensor(stat[:, par, 6:7], stat[:, par, 3:4], ln_const[:, 2:3], ALU.add).then_inc(ln_p, 1)
            pool.wait_ge(ln_p, 5 * idx + 3)
            nc.gpsimd.tensor_tensor(stat[:, par, 4:5], stat[:, par, 6:7], expo[:, 0:1], ALU.pow).then_inc(ln_p, 1)
            pool.wait_ge(ln_p, 5 * idx + 4)
            nc.gpsimd.tensor_tensor(stat[:, par, 5:6], stat[:, par, 1:2], stat[:, par, 4:5],
                                    ALU.mult).then_inc(ln_p, 1)

        with phase_semaphores(nc) as s:
            loaded, idz, made, w12, cdone = (s(n) for n in (
                "c_loaded", "c_ident_zero", "c_made", "c_w12", "c_copied"))
            with nc.Block() as block:
                @block.sync
                def _(sp):
                    chunked = lambda w: w.rearrange("(c p) f -> p c f", p=P)
                    loads = [(wqk[:, :, 0:A], chunked(A3)), (a1t, A1T.rearrange("a (c p) -> a c p", p=P)),
                             (a2, A2), (ua[:], chunked(UA)), (ub[:], chunked(UB)), (uc[:], chunked(UC)),
                             (bias0[:], b0.partition_broadcast(P)), (gam[:], gamma.partition_broadcast(P)),
                             (bet[:], beta.partition_broadcast(P)), (tb[:], tin.partition_broadcast(P))]
                    for dst, src in loads:
                        sp.dma_start(dst, src).then_inc(loaded, 16)
                    sp.wait_ge(loaded, 16 * len(loads))

                @block.gpsimd
                def _(pool):
                    nc.gpsimd.memset(ident[:], 0.0).then_inc(idz, 1)
                    nc.gpsimd.memset(ones[:], 1.0)
                    nc.gpsimd.memset(expo[:], -0.5)
                    for i, value in enumerate((-1.0 / D, 1.0 / D, LN_EPS)):
                        nc.gpsimd.memset(ln_const[:, i:i + 1], value)
                    nc.gpsimd.memset(zero[:], 0.0)
                    pool.wait_ge(idz, 1)
                    nc.gpsimd.affine_select(out=ident[:], in_=ident[:], compare_op=ALU.not_equal, fill=1.0, base=0,
                                            pattern=[[-1, P]], channel_multiplier=1).then_inc(made, 1)

                @block.tensor
                def _(pe):
                    pe.wait_ge(loaded, 16 * 10)
                    for c in range(DC):
                        last = nc.tensor.matmul(misc[:, c * A:(c + 1) * A], a1t[:, c, :], a2, start=True, stop=True)
                    last.then_inc(w12, 1)

                @block.vector
                def _(dve):
                    dve.wait_ge(w12, 1)
                    nc.vector.tensor_copy(wqk[:, :, A:2 * A],
                                          misc[:, 0:DC * A].rearrange("p (c a) -> p c a", c=DC)).then_inc(cdone, 1)
                    dve.wait_ge(loaded, 16 * 10)
                    nc.vector.tensor_scalar(omt[:], tb[:], -1.0, 1.0, ALU.mult, ALU.add).then_inc(cdone, 1)

                @block.scalar
                def _(act):
                    act.wait_ge(cdone, 2)

        def layer(name, src_t, rowsum=False, rhs=None, plus_self=True, evac=None, dst_t=None,
                  nxt=None, weight=None, hnext=None, colsum=False):
            two_stage = nxt is not None
            use_adj = rowsum or rhs is not None
            with phase_semaphores(nc, name + "_") as s:
                weight_in = s("weight_in")
                adj_in = [s("adj_in0"), s("adj_in1")]
                x_in = [s("x_in0"), s("x_in1")]
                x_out = [s("x_out0"), s("x_out1")]
                agg_done, agg_copied, summed = s("agg_done"), s("agg_copied"), s("col_summed")
                pre, xnew = s("pre_added"), s("x_new")
                normed, transposed, hT_ready, dense_done, dense_copied = (
                    s("normed"), s("transposed"), s("hT_ready"), s("dense_done"), s("dense_copied"))
                h_kept, rs_ready = s("h_kept"), s("rs_ready")
                ln = (s("ln_act"), s("ln_pool"))
                acc = banks[4:6]
                xsrc = xt if evac is None else xn

                with nc.Block() as block:
                    @block.sync
                    def _(sp):
                        def body(u, par, live):
                            if live[0] and use_adj:
                                if not isinstance(u, int) or u >= 2:
                                    sp.wait_ge(agg_done, u - 1)
                                    if colsum:
                                        sp.wait_ge(summed, u - 1)
                                src = adjR[u].rearrange("i (j q) -> i j q", q=P) if rowsum else adjT[u]
                                sp.dma_start(adj[:, par], src).then_inc(adj_in[par], 16)
                            if live[0]:
                                if not isinstance(u, int) or u >= 2:
                                    if evac is None:
                                        sp.wait_ge(normed, u - 1)
                                    else:
                                        sp.wait_ge(xnew, u - 1)
                                sp.dma_start(xt[:, par], src_t[u]).then_inc(x_in[par], 16)
                            if live[1] and evac is not None:
                                sp.wait_ge(xnew, u)
                                sp.dma_start(dst_t[u - 1], xn[:, 1 - par]).then_inc(x_out[1 - par], 16)
                        if weight is not None:
                            sp.dma_start(wd[:], weight.rearrange("(c p) f -> p c f", p=P)).then_inc(weight_in, 16)
                        pipeline(sp, NT, body)
                        if evac is not None:
                            for par in range(2):
                                sp.wait_ge(x_out[par], 16 * (NT // 2))

                    @block.tensor
                    def _(pe):
                        def body(u, par, live):
                            if live[2] and two_stage:
                                pe.wait_ge(normed, u - 1)
                                if not isinstance(u, int) or u >= 3:
                                    pe.wait_ge(hT_ready, u - 2)
                                for c in range(DC):
                                    last = nc.tensor.transpose(misc[:, c * P:(c + 1) * P], cc[:, par, c * P:(c + 1) * P],
                                                               ident[:])
                                last.then_inc(transposed, 1)
                            if live[0] and rhs is not None:
                                pe.wait_ge(adj_in[par], 8 * u + (16 if par == 0 else 8))
                                if not isinstance(u, int) or u >= 2:
                                    pe.wait_ge(agg_copied, u - 1)
                                for j in range(NT):
                                    last = nc.tensor.matmul(acc[par][:, 0:D], adj[:, par, j], rhs[:, j],
                                                            start=(j == 0), stop=(j == NT - 1 and not plus_self))
                                if plus_self:
                                    last = nc.tensor.matmul(acc[par][:, 0:D], ident[:], rhs[:, u],
                                                            start=False, stop=True)
                                last.then_inc(agg_done, 1)
                            if live[2] and two_stage:
                                pe.wait_ge(hT_ready, u - 1)
                                if not isinstance(u, int) or u >= 3:
                                    pe.wait_ge(dense_copied, u - 2)
                                for c in range(DC):
                                    if nxt == "dense":
                                        last = nc.tensor.matmul(dense[:, 0:D], hT[:, c], wd[:, c],
                                                                start=(c == 0), stop=(c == DC - 1))
                                    else:
                                        last = nc.tensor.matmul(dense[:, 0:P], wqk[:, c], hT[:, c],
                                                                start=(c == 0), stop=(c == DC - 1))
                                last.then_inc(dense_done, 1)
                        if weight is not None:
                            pe.wait_ge(weight_in, 16)
                        pipeline(pe, NT, body)

                    @block.scalar
                    def _(act):
                        def body(u, par, live):
                            if live[2] and two_stage:
                                act.wait_ge(transposed, u - 1)
                                if not isinstance(u, int) or u >= 3:
                                    act.wait_ge(dense_done, u - 2)
                                nc.scalar.activation(hT[:].rearrange("p c i -> p (c i)"), misc[:, 0:D],
                                                     ACT.Copy).then_inc(hT_ready, 1)
                            if live[0] and evac is not None:
                                act.wait_ge(agg_done, u + 1)
                                if not isinstance(u, int) or u >= 2:
                                    act.wait_ge(xnew, u - 1)
                                if evac == "layer0":
                                    nc.scalar.activation(t0[:, par], acc[par][:, 0:D], ACT.Copy,
                                                         scale=d0[:, bass.ds(u, 1)]).then_inc(agg_copied, 1)
                                elif evac == "layer1":
                                    nc.scalar.activation(t0[:, par], acc[par][:, 0:D], ACT.Relu,
                                                         scale=d1[:, bass.ds(u, 1)]).then_inc(agg_copied, 1)
                                else:
                                    nc.scalar.activation(t1[:, par], rhs[:, u], ACT.Copy, scale=omt[:])
                                    nc.scalar.activation(t0[:, par], acc[par][:, 0:D], ACT.Copy,
                                                         scale=tb[:]).then_inc(agg_copied, 1)
                            if live[0] and two_stage:
                                if evac is None:
                                    act.wait_ge(x_in[par], 8 * u + (16 if par == 0 else 8))
                                else:
                                    act.wait_ge(xnew, u + 1)
                                if not isinstance(u, int) or u >= 2:
                                    act.wait_ge(transposed, u - 1)
                                    if nxt == "attention":
                                        act.wait_ge(h_kept, u - 1)
                                ln_act(act, ln, u, par, xsrc[:, par], cc[:, par], ACT.Relu).then_inc(normed, 1)
                        pipeline(act, NT, body)

                    @block.gpsimd
                    def _(pool):
                        def body(u, par, live):
                            if live[0] and evac is not None:
                                pool.wait_ge(x_in[par], 8 * u + (16 if par == 0 else 8))
                                if not isinstance(u, int) or u >= 2:
                                    pool.wait_ge(x_out[par], 8 * u + (0 if par == 0 else -8))
                                    if two_stage:
                                        pool.wait_ge(normed, u - 1)
                                if evac == "layer0":
                                    nc.gpsimd.tensor_tensor(xt[:, par], xt[:, par], bias0[:], ALU.add).then_inc(pre, 1)
                                    pool.wait_ge(pre, u + 1)
                                    pool.wait_ge(agg_copied, u + 1)
                                elif evac == "layer1":
                                    pool.wait_ge(agg_copied, u + 1)
                                else:
                                    pool.wait_ge(agg_copied, u + 1)
                                    nc.gpsimd.tensor_tensor(xt[:, par], xt[:, par], t1[:, par], ALU.add).then_inc(pre, 1)
                                    pool.wait_ge(pre, u + 1)
                                nc.gpsimd.tensor_tensor(xn[:, par], xt[:, par], t0[:, par], ALU.add).then_inc(xnew, 1)
                            if live[0] and two_stage:
                                ln_pool(pool, ln, u, par)
                            if live[0] and nxt == "attention":
                                pool.wait_ge(normed, u + 1)
                                nc.gpsimd.tensor_copy(Hc[:, u], cc[:, par]).then_inc(h_kept, 1)
                        pipeline(pool, NT, body)

                    @block.vector
                    def _(dve):
                        def body(u, par, live):
                            if live[0] and rowsum:
                                dve.wait_ge(adj_in[par], 8 * u + (16 if par == 0 else 8))
                                nc.vector.reduce_sum(rs[:, bass.ds(u, 1)], adj[:, par].rearrange("i j q -> i (j q)"),
                                                     axis=AX_X).then_inc(agg_done, 1)
                            if live[0] and colsum:
                                dve.wait_ge(adj_in[par], 8 * u + (16 if par == 0 else 8))
                                if not isinstance(u, int) or u >= 2:
                                    dve.wait_ge(csadd, u - 1)
                                nc.vector.reduce_sum(cpart[:, par], adj[:, par], axis=AX_X).then_inc(summed, 1)
                                dve.wait_ge(summed, u + 1)
                                if not isinstance(u, int) or u >= 1:
                                    dve.wait_ge(csadd, u)
                                if isinstance(u, int) and u == 0:
                                    nc.vector.tensor_scalar(cs[:], cpart[:, par], 1.0, None, ALU.add).then_inc(csadd, 1)
                                else:
                                    nc.vector.tensor_tensor(cs[:], cs[:], cpart[:, par], ALU.add).then_inc(csadd, 1)
                            if live[2] and two_stage:
                                dve.wait_ge(dense_done, u - 1)
                                if nxt == "attention":
                                    nc.vector.tensor_copy(qk[:, bass.ds((u - 2) * P, P)],
                                                          dense[:, 0:P]).then_inc(dense_copied, 1)
                                elif evac is None:
                                    nc.vector.tensor_copy(hnext[:, u - 2], dense[:, 0:D]).then_inc(dense_copied, 1)
                                else:
                                    nc.vector.tensor_scalar(hnext[:, u - 2], dense[:, 0:D], d1[:, bass.ds(u - 2, 1)], None,
                                                            ALU.mult).then_inc(dense_copied, 1)
                        csadd = s("cs_added")
                        pipeline(dve, NT, body)
                        if rowsum:
                            dve.wait_ge(agg_done, NT)
                            nc.vector.tensor_scalar(rs[:], rs[:], 1.0, None, ALU.add).then_inc(agg_copied, 1)
                            dve.wait_ge(agg_copied, 1)
                        if colsum:
                            dve.wait_ge(csadd, NT)
                            nc.vector.tensor_scalar(cs[:], cs[:], CLIP, None, ALU.max).then_inc(csadd, 1)
                            dve.wait_ge(csadd, NT + 1)
                            nc.vector.reciprocal(ic[:], cs[:]).then_inc(csadd, 1)
                            dve.wait_ge(csadd, NT + 2)

        xz = sb("xz", [P, 2, D])

        layer("rowsum", xin_t, rowsum=True, nxt="dense", weight=W0T, hnext=Ha)

        with phase_semaphores(nc) as s:
            powd, fin = s("n_pow"), s("n_fin")
            with nc.Block() as block:
                @block.gpsimd
                def _(pool):
                    nc.gpsimd.tensor_tensor(d0[:], rs[:], expo[:], ALU.pow).then_inc(powd, 1)

                @block.vector
                def _(dve):
                    nc.vector.tensor_scalar(dinf[:], rs[:], 0.0, None, ALU.is_equal).then_inc(fin, 1)
                    nc.vector.tensor_scalar(ir[:], rs[:], CLIP, None, ALU.max).then_inc(fin, 1)
                    dve.wait_ge(powd, 1)
                    nc.vector.tensor_copy(d1[:], d0[:]).then_inc(fin, 1)
                    dve.wait_ge(fin, 3)
                    nc.vector.copy_predicated(d1[:], dinf[:], zero[:]).then_inc(fin, 1)
                    nc.vector.reciprocal(ir[:], ir[:]).then_inc(fin, 1)
                    for j in range(NT):
                        nc.vector.tensor_scalar(Ha[:, j], Ha[:, j], d0[:, j:j + 1], None, ALU.mult).then_inc(fin, 1)
                    dve.wait_ge(fin, 5 + NT)

        layer("layer0", xin_t, rhs=Ha, evac="layer0", dst_t=x1_t, nxt="dense", weight=W1g, hnext=Hb, colsum=True)
        layer("layer1", x1_t, rhs=Hb, evac="layer1", dst_t=x2_t, nxt="attention")

        with ExitStack() as att:
            ab = lambda name, shape, dt=F32: att.enter_context(nc.sbuf_tensor(name, shape, dt))
            E = ab("E", [P, 2, NP])
            U = ab("U", [P, NPAD])
            PT = ab("PT", [P, NT, P])
            qt = ab("qt", [A, 2, P])
            g = bias0
            gT, xaT = (wd[:, i].rearrange("p (c i) -> p c i", c=DC) for i in range(2))
            gTf, xaTf = wd[:, 0], wd[:, 1]
            qkb = hT
            nmax = ab("nmax", [P, 2])
            Zs = ab("Zs", [P, 2])
            rz = ab("rz", [P, 2])
            NF = max(map(len, FIXED))
            over_all = ab("over", [P, 2, NF])
            sign_all = ab("sign", [P, 2, NF])
            neg_c_all = ab("neg_c", [P, NF])
            neg_3c_all = ab("neg_3c", [P, NF])
            half_c_all = ab("half_c", [P, NF])
            half_nc_all = ab("half_nc", [P, NF])
            table_all = ab("table", [P, NF + 2, 3])
            ft_all = ab("ft", [P, 2, NF])
            met_all = ab("met", [P, NF + 2])
            pick_all = ab("pick", [P, NF + 1])
            both_all = ab("both", [P, 2, NF + 1, 3])
            share = ab("share", [P, 4])
            tgt2 = ab("tgt2", [P, 2])
            ends2 = ab("ends2", [P, 2, 2, 3])
            new2 = ab("new2", [P, 2, 3])
            sp_ = ab("sp_", [P, 8])
            up = ab("up", [P, 3], I32)
            down = ab("down", [P, 3], I32)
            sc = ab("sc", [P, 8])
            keep = ab("keep", [P, TOP], I32)
            top8 = ab("top8", [P, TOP])
            mark = ab("mark", [P, TOP])
            mass = ab("mass", [P, TOP + 1])
            kmass = ab("kmass", [P, TOP])
            ones8 = ab("ones8", [P, TOP])
            flag = ab("flag", [P, 32])
            flagT = ab("flagT", [P, 32])
            flagm = ab("flagm", [P, 1])
            flagi = ab("flagi", [P, 1], I32)

            for step in range(2):
                with phase_semaphores(nc, f"att{step}_") as s:
                    adj_in = [s("adj_in0"), s("adj_in1")]
                    ops_in = s("operands_in")
                    x_in = [s("x_in0"), s("x_in1")]
                    z_out = [s("z_out0"), s("z_out1")]
                    q_ready, lg_done, lg_copied = s("q_ready"), s("lg_done"), s("lg_copied")
                    tr_done, pt_copied = s("tr_done"), s("pt_copied")
                    max_ready, exp_done, probs_ready = s("max_ready"), s("exp_done"), s("probs_ready")
                    agg_done, agg_copied, ax_done, ax_copied = (
                        s("agg_done"), s("agg_copied"), s("ax_done"), s("ax_copied"))
                    g_ready, gT_done, gT_ready = s("g_ready"), s("gT_done"), s("gT_ready")
                    xa_ready, xT_done, xT_ready = s("xa_ready"), s("xT_done"), s("xT_ready")
                    ua_done, ua_copied, ub_done = s("ua_done"), s("ua_copied"), s("ub_done")
                    uc_done, qk_done, qk_copied = s("uc_done"), s("qk_done"), s("qk_copied")
                    z_part, z_mid, z_done = s("z_part"), s("z_mid"), s("z_done")
                    ln = (s("ln_act"), s("ln_pool"))
                    y_ready, c_ready, x_pre = s("y_ready"), s("c_ready"), s("x_pre")
                    search, rnd, fixed_done, consts = s("search_step"), s("round_step"), s("fixed_done"), s("consts")
                    init, bracketed, searched = s("bracket_step"), s("bracketed"), s("searched")
                    V = big
                    zo = xt if step == 0 else xz
                    NF = len(FIXED[step])
                    over, sign, ft = (a[:, :, 0:NF] for a in (over_all, sign_all, ft_all))
                    neg_c, neg_3c, half_c, half_nc = (a[:, 0:NF] for a in (neg_c_all, neg_3c_all, half_c_all, half_nc_all))
                    table, met, pick = table_all[:, 0:NF + 2], met_all[:, 0:NF + 2], pick_all[:, 0:NF + 1]
                    both = both_all[:, :, 0:NF + 1]
                    later = lambda u, k: not isinstance(u, int) or u >= k
                    slot = lambda t, par: 8 * t + (16 if par == 0 else 8)

                    with nc.Block() as block:
                        @block.sync
                        def _(sp):
                            if step == 1:
                                sp.dma_start(qk[:].rearrange("p (t i) -> p t i", i=P),
                                             qk_d.rearrange("t p i -> p t i")).then_inc(ops_in, 16)
                                sp.dma_start(Hc[:], v3_d.rearrange("t p c -> p t c")).then_inc(ops_in, 16)

                            def body(u, par, live):
                                if live[0]:
                                    if later(u, 2):
                                        sp.wait_ge(agg_done, u - 1)
                                    sp.dma_start(adj[:, par], adjT[u]).then_inc(adj_in[par], 16)
                                if step == 0 and live[2]:
                                    sp.wait_ge(z_done, u - 1)
                                    sp.dma_start(z_t[u - 2], zo[:, par]).then_inc(z_out[par], 16)
                                    sp.wait_ge(ax_copied, u - 1)
                                    sp.dma_start(v3_d[u - 2], xn[:, par]).then_inc(z_out[par], 16)
                                    sp.wait_ge(qk_copied, u - 1)
                                    sp.dma_start(qk_d[u - 2], qkb[:, par]).then_inc(z_out[par], 16)
                                if step == 1 and live[1]:
                                    if later(u, 3):
                                        sp.wait_ge(z_done, u - 2)
                                    sp.dma_start(xt[:, 1 - par], z_t[u - 1]).then_inc(x_in[1 - par], 16)
                                    sp.dma_start(xn[:, 1 - par], x2_t[u - 1]).then_inc(x_in[1 - par], 16)
                                if step == 1 and live[2]:
                                    sp.wait_ge(z_done, u - 1)
                                    sp.dma_start(x3_t[u - 2], zo[:, par]).then_inc(z_out[par], 16)
                            pipeline(sp, NT, body)
                            for par in range(2):
                                sp.wait_ge(z_out[par], 16 * (3 if step == 0 else 1) * (NT // 2))

                        @block.tensor
                        def _(pe):
                            if step == 1:
                                pe.wait_ge(ops_in, 32)

                            def body(u, par, live):
                                for k, (c0, cw) in enumerate(CHUNKS):
                                    ring = (par * KC + k) % 2
                                    if live[2]:
                                        if k == 0:
                                            pe.wait_ge(probs_ready, u - 1)
                                        if later(u, 3) or k >= 2:
                                            pe.wait_ge(pt_copied, KC * (u - 2) + k - 1)
                                        for i in range(cw // P):
                                            last = nc.tensor.transpose(tr[ring][:, i * P:(i + 1) * P],
                                                                       E[:, par, c0 + i * P:c0 + (i + 1) * P], ident[:])
                                        last.then_inc(tr_done, 1)
                                    if live[0]:
                                        if k == 0:
                                            pe.wait_ge(q_ready, u + 1)
                                        if later(u, 1) or k >= 2:
                                            pe.wait_ge(lg_copied, KC * u + k - 1)
                                        nc.tensor.matmul(lg[ring][:, 0:cw], qt[:, par], qk[0:A, c0:c0 + cw],
                                                         start=True, stop=True).then_inc(lg_done, 1)
                                if live[1]:
                                    q = 1 - par
                                    pe.wait_ge(adj_in[q], slot(u - 1, q))
                                    if later(u, 2):
                                        pe.wait_ge(agg_copied, u - 1)
                                    rhs = Hc if step == 0 else V
                                    w = D if step == 0 else 2 * D
                                    for j in range(NT):
                                        nc.tensor.matmul(agg[:, 0:w], adj[:, q, j], rhs[:, j], start=(j == 0), stop=False)
                                    nc.tensor.matmul(agg[:, 0:w], ident[:], rhs[:, u - 1],
                                                     start=False, stop=True).then_inc(agg_done, 1)
                                if live[2]:
                                    if later(u, 3):
                                        pe.wait_ge(ax_copied, u - 2)
                                    for k, (c0, cw) in enumerate(CHUNKS):
                                        pe.wait_ge(pt_copied, KC * (u - 2) + k + 1)
                                        for j in range(c0 // P, (c0 + cw) // P):
                                            last = nc.tensor.matmul(axp[:, 0:D], PT[:, j], Hc[:, j],
                                                                    start=(j == 0), stop=(j == NT - 1))
                                    last.then_inc(ax_done, 1)
                                if step == 1:
                                    return
                                if live[1]:
                                    pe.wait_ge(g_ready, u)
                                    if later(u, 3):
                                        pe.wait_ge(qk_copied, u - 2)
                                    for c in range(DC):
                                        last = nc.tensor.transpose(misc[:, c * P:(c + 1) * P], g[:, c * P:(c + 1) * P],
                                                                   ident[:])
                                    last.then_inc(gT_done, 1)
                                if live[2]:
                                    pe.wait_ge(xa_ready, u - 1)
                                    pe.wait_ge(ua_copied, u - 1)
                                    for c in range(DC):
                                        last = nc.tensor.transpose(dense[:, c * P:(c + 1) * P],
                                                                   cc[:, par, c * P:(c + 1) * P], ident[:])
                                    last.then_inc(xT_done, 1)
                                if live[1]:
                                    pe.wait_ge(gT_ready, u)
                                    if live[2]:
                                        pe.wait_ge(xT_ready, u - 1)
                                    for bank, wt, done in ((dense, ua, ua_done), (agg, ub, ub_done)):
                                        for c in range(DC):
                                            last = nc.tensor.matmul(bank[:, 0:2 * D], gT[:, c], wt[:, c],
                                                                    start=(c == 0), stop=(c == DC - 1))
                                        last.then_inc(done, 1)
                                if live[2]:
                                    pe.wait_ge(xT_ready, u - 1)
                                    for c in range(DC):
                                        last = nc.tensor.matmul(axp[:, 0:2 * D], xaT[:, c], uc[:, c],
                                                                start=(c == 0), stop=(c == DC - 1))
                                    last.then_inc(uc_done, 1)
                                    for c in range(DC):
                                        last = nc.tensor.matmul(misc[:, 0:P], wqk[:, c], xaT[:, c],
                                                                start=(c == 0), stop=(c == DC - 1))
                                    last.then_inc(qk_done, 1)
                            pipeline(pe, NT, body)

                        @block.scalar
                        def _(act):
                            act.wait_ge(consts, 1)
                            if step == 1:
                                act.wait_ge(ops_in, 32)

                            def fixed_sums(u, par, part):
                                sums = [(func, c, acc_) for c in range(NF) for func, acc_ in ((ACT.Relu, over), (ACT.Sign, sign))]
                                mine = sums[:NF] if part == 0 else sums[NF:]
                                for i, (func, c, acc_) in enumerate(mine):
                                    act.wait_ge(fixed_done, 2 * NF * u + NF * part + i)
                                    less, scale = (neg_3c, 3.0) if func == ACT.Sign else (neg_c, 1.0)
                                    nc.scalar.activation(junk[:, 0:N], E[:, par, 0:N], func, bias=less[:, c:c + 1],
                                                         scale=scale, accum_out=acc_[:, par, c:c + 1]).then_inc(fixed_done, 1)

                            def body(u, par, live):
                                q = 1 - par
                                if live[0]:
                                    if later(u, 2):
                                        act.wait_ge(lg_done, KC * (u - 1))
                                    nc.scalar.activation(qt[:, par], qk[A:2 * A, bass.ds(u * P, P)],
                                                         ACT.Copy).then_inc(q_ready, 1)
                                for k, (c0, cw) in enumerate(CHUNKS):
                                    ring = (par * KC + k) % 2
                                    if live[2]:
                                        act.wait_ge(tr_done, KC * (u - 2) + k + 1)
                                        if k == 0 and later(u, 3):
                                            act.wait_ge(ax_done, u - 2)
                                        nc.scalar.activation(PT[:].rearrange("p t i -> p (t i)")[:, c0:c0 + cw],
                                                             tr[ring][:, 0:cw], ACT.Copy).then_inc(pt_copied, 1)
                                    if live[0]:
                                        act.wait_ge(lg_done, KC * u + k + 1)
                                        nc.scalar.activation(E[:, par, c0:c0 + cw], lg[ring][:, 0:cw],
                                                             ACT.Copy).then_inc(lg_copied, 1)
                                if live[0]:
                                    act.wait_ge(max_ready, u + 1)
                                    act.wait_ge(lg_copied, KC * (u + 1))
                                    nc.scalar.activation(E[:, par, 0:N], E[:, par, 0:N], ACT.Exp, bias=nmax[:, par:par + 1],
                                                         accum_out=Zs[:, par:par + 1]).then_inc(exp_done, 1)
                                    act.wait_ge(exp_done, u + 1)
                                    fixed_sums(u, par, 0)
                                    if step == 1:
                                        fixed_sums(u, par, 1)
                                if step == 0:
                                    if live[1]:
                                        act.wait_ge(agg_done, u)
                                        nc.scalar.activation(g[:], agg[:, 0:D], ACT.Copy).then_inc(g_ready, 1)
                                    if live[0]:
                                        fixed_sums(u, par, 1)
                                    if live[2]:
                                        act.wait_ge(ax_done, u - 1)
                                        nc.scalar.activation(cc[:, par], axp[:, 0:D], ACT.Copy,
                                                             scale=rz[:, par:par + 1]).then_inc(xa_ready, 1)
                                    if live[1]:
                                        act.wait_ge(gT_done, u)
                                        nc.scalar.activation(gTf, misc[:, 0:D],
                                                             ACT.Copy).then_inc(gT_ready, 1)
                                    if live[2]:
                                        act.wait_ge(xT_done, u - 1)
                                        nc.scalar.activation(xaTf, dense[:, 0:D],
                                                             ACT.Copy).then_inc(xT_ready, 1)
                                    if live[1]:
                                        act.wait_ge(ua_done, u)
                                        if later(u, 3):
                                            act.wait_ge(z_part, u - 2)
                                        nc.scalar.activation(t0[:, q], dense[:, 0:D], ACT.Copy, scale=ir[:, bass.ds(u - 1, 1)])
                                        nc.scalar.activation(t1[:, q], dense[:, D:2 * D], ACT.Copy,
                                                             scale=ic[:, bass.ds(u - 1, 1)]).then_inc(ua_copied, 1)
                                        act.wait_ge(ub_done, u)
                                        nc.scalar.activation(V[:, u - 1, 0:D], agg[:, 0:D], ACT.Copy,
                                                             scale=ir[:, bass.ds(u - 1, 1)])
                                        nc.scalar.activation(V[:, u - 1, D:2 * D], agg[:, D:2 * D], ACT.Copy,
                                                             scale=ic[:, bass.ds(u - 1, 1)]).then_inc(agg_copied, 1)
                                    if live[2]:
                                        act.wait_ge(uc_done, u - 1)
                                        if later(u, 4):
                                            act.wait_ge(z_out[par], 24 * (u - 2) + (0 if par == 0 else -24))
                                            act.wait_ge(z_done, u - 3)
                                        nc.scalar.activation(xt[:, par], axp[:, 0:D], ACT.Copy)
                                        nc.scalar.activation(xn[:, par], axp[:, D:2 * D], ACT.Copy).then_inc(ax_copied, 1)
                                        act.wait_ge(qk_done, u - 1)
                                        nc.scalar.activation(qkb[:, par], misc[:, 0:P], ACT.Copy).then_inc(qk_copied, 1)
                                else:
                                    if live[1]:
                                        act.wait_ge(agg_done, u)
                                        if later(u, 3):
                                            act.wait_ge(z_part, u - 2)
                                        nc.scalar.activation(t0[:, q], agg[:, 0:D], ACT.Copy, scale=ir[:, bass.ds(u - 1, 1)])
                                        nc.scalar.activation(t1[:, q], agg[:, D:2 * D], ACT.Copy,
                                                             scale=ic[:, bass.ds(u - 1, 1)]).then_inc(agg_copied, 1)
                                    if live[2]:
                                        act.wait_ge(ax_done, u - 1)
                                        if later(u, 3):
                                            act.wait_ge(y_ready, u - 2)
                                        nc.scalar.activation(g[:], axp[:, 0:D], ACT.Copy,
                                                             scale=rz[:, par:par + 1]).then_inc(ax_copied, 1)
                                        act.wait_ge(y_ready, u - 1)
                                        if later(u, 4):
                                            act.wait_ge(z_done, u - 3)
                                        ln_act(act, ln, u - 2, par, xt[:, par], cc[:, par], ACT.Identity).then_inc(c_ready, 1)
                            pipeline(act, NT, body)

                        @block.gpsimd
                        def _(pool):
                            G_ = nc.gpsimd
                            values = [(table[:, 0], 0.0), (table[:, NF + 1, 0:1], 1.5), (table[:, NF + 1, 1:3], 0.0),
                                      (met[:, 0:1], 1.0), (met[:, NF + 1:NF + 2], 0.0)]
                            for i, value in enumerate(FIXED[step]):
                                c, _ = between_floats(value)
                                values += [(table[:, i + 1, 0:1], c), (half_c[:, i:i + 1], c / 2),
                                           (half_nc[:, i:i + 1], c * N / 2)]
                            for i, value in enumerate((P_NUC, 1 - P_NUC, -P_NUC, -1.0)):
                                values.append((share[:, i:i + 1], value))
                            for dst, value in values:
                                G_.memset(dst, value).then_inc(init, 1)
                            pool.wait_ge(init, len(values))
                            pool.sem_clear(init)

                            def bracket(t, par):
                                n = [0]

                                def then(*ins):
                                    for i in ins:
                                        i.then_inc(init, 1)
                                    n[0] += len(ins)
                                    pool.wait_ge(init, n[0])
                                tt = G_.tensor_tensor
                                tgt, new = tgt2[:, par:par + 1], new2[:, par]
                                lo, hi = ends2[:, par, 0], ends2[:, par, 1]
                                mid = table[:, 1:NF + 1]
                                pool.wait_ge(fixed_done, 2 * NF * (t + 1))
                                if later(t, 2):
                                    pool.wait_ge(searched, t - 1)
                                then(tt(ft[:, 0], sign[:, par], half_c, ALU.mult),
                                     tt(ft[:, 1], over[:, par], half_nc, ALU.add),
                                     tt(tgt, Zs[:, par:par + 1], share[:, 0:1], ALU.mult),
                                     tt(table[:, 0, 1:2], Zs[:, par:par + 1], share[:, 1:2], ALU.mult),
                                     tt(table[:, NF + 1, 1:2], Zs[:, par:par + 1], share[:, 2:3], ALU.mult))
                                then(tt(mid[:, :, 2], ft[:, 0], ft[:, 1], ALU.add))
                                then(tt(mid[:, :, 1], mid[:, :, 2], tgt.to_broadcast([P, NF]), ALU.subtract),
                                     G_.tensor_scalar(met[:, 1:NF + 1], mid[:, :, 2], tgt, None, ALU.is_ge))
                                for i in range(2, NF + 1):
                                    then(tt(met[:, i:i + 1], met[:, i:i + 1], met[:, i - 1:i], ALU.mult))
                                then(tt(pick, met[:, 0:NF + 1], met[:, 1:NF + 2], ALU.subtract))
                                w = pick.unsqueeze(2).to_broadcast([P, NF + 1, 3])
                                then(tt(both[:, 0], table[:, 0:NF + 1], w, ALU.mult),
                                     tt(both[:, 1], table[:, 1:NF + 2], w, ALU.mult))
                                for i in range(1, NF):
                                    then(tt(both[:, :, 0], both[:, :, 0], both[:, :, i], ALU.add))
                                then(tt(ends2[:, par], both[:, :, 0], both[:, :, NF], ALU.add))
                                then(tt(sp_[:, 0:1], lo[:, 1:2], hi[:, 1:2], ALU.subtract),
                                     tt(sp_[:, 1:2], hi[:, 0:1], lo[:, 0:1], ALU.subtract))
                                then(tt(sp_[:, 2:3], sp_[:, 0:1], share[:, 3:4], ALU.pow),
                                     tt(sp_[:, 3:4], sp_[:, 1:2], lo[:, 1:2], ALU.mult))
                                then(tt(sp_[:, 4:5], sp_[:, 2:3], sp_[:, 3:4], ALU.mult))
                                then(tt(new[:, 0:1], sp_[:, 4:5], lo[:, 0:1], ALU.add))
                                pool.sem_inc(bracketed, 1)
                                pool.sem_clear(init)

                            def body(u, par, live):
                                q = 1 - par
                                if live[0]:
                                    bracket(u, par)
                                if step == 0:
                                    if live[1]:
                                        pool.wait_ge(ua_copied, u)
                                        nc.gpsimd.tensor_tensor(t0[:, q], t0[:, q], t1[:, q], ALU.add).then_inc(z_mid, 1)
                                        pool.wait_ge(z_mid, u)
                                        if later(u, 3):
                                            pool.wait_ge(z_done, u - 2)
                                        nc.gpsimd.tensor_tensor(xz[:, q], t0[:, q], Hc[:, u - 1], ALU.add).then_inc(z_part, 1)
                                    if live[2]:
                                        pool.wait_ge(ax_copied, u - 1)
                                        pool.wait_ge(z_part, u - 1)
                                        nc.gpsimd.tensor_tensor(zo[:, par], xz[:, par], xt[:, par], ALU.add).then_inc(z_done, 1)
                                else:
                                    if live[1]:
                                        pool.wait_ge(agg_copied, u)
                                        nc.gpsimd.tensor_tensor(t0[:, q], t0[:, q], t1[:, q], ALU.add).then_inc(z_mid, 1)
                                        pool.wait_ge(z_mid, u)
                                        pool.wait_ge(x_in[q], 2 * slot(u - 1, q))
                                        nc.gpsimd.tensor_tensor(xt[:, q], xt[:, q], t0[:, q], ALU.add).then_inc(z_part, 1)
                                    if live[2]:
                                        pool.wait_ge(ax_copied, u - 1)
                                        pool.wait_ge(z_part, u - 1)
                                        nc.gpsimd.tensor_tensor(xt[:, par], xt[:, par], g[:], ALU.add).then_inc(y_ready, 1)
                                        nc.gpsimd.tensor_tensor(xn[:, par], xn[:, par], bet[:], ALU.add).then_inc(x_pre, 1)
                                        ln_pool(pool, ln, u - 2, par)
                                        pool.wait_ge(c_ready, u - 1)
                                        nc.gpsimd.tensor_tensor(cc[:, par], cc[:, par], gam[:], ALU.mult).then_inc(x_pre, 1)
                                        pool.wait_ge(x_pre, 2 * (u - 1))
                                        if later(u, 4):
                                            pool.wait_ge(z_out[par], 8 * (u - 2) + (0 if par == 0 else -8))
                                        nc.gpsimd.tensor_tensor(zo[:, par], xn[:, par], cc[:, par],
                                                                ALU.add).then_inc(z_done, 1)
                            pipeline(pool, NT, body)

                        @block.vector
                        def _(dve):
                            V_ = nc.vector
                            more = dve.alloc_register(f"rounds_end{step}")
                            open_rows = [dve.alloc_register(f"open{step}_{i}") for i in range(4)]
                            V_.memset(ones8[:], 1.0)
                            for i, value in enumerate(FIXED[step]):
                                c, three_c = between_floats(value)
                                V_.memset(neg_c[:, i:i + 1], -c)
                                V_.memset(neg_3c[:, i:i + 1], -three_c)
                            V_.memset(flag[:], 0.0).then_inc(search, 1)
                            dve.wait_ge(search, 1)
                            dve.sem_inc(consts, 1)

                            def body(u, par, live):
                                q = 1 - par
                                count = [0]

                                def then(*ins):
                                    for i in ins:
                                        i.then_inc(search, 1)
                                    count[0] += len(ins)
                                    dve.wait_ge(search, count[0])

                                dve.sem_clear(search)

                                def row_max():
                                    dve.wait_ge(lg_copied, KC * (u + 1))
                                    if later(u, 2):
                                        dve.wait_ge(exp_done, u - 1)
                                    V_.tensor_reduce(nmax[:, par:par + 1], E[:, par, 0:N], axis=AX_X, op=ALU.max,
                                                     negate=True).then_inc(max_ready, 1)
                                if not live[1]:
                                    if live[0]:
                                        row_max()
                                    return
                                e = E[:, q, 0:N]
                                dve.wait_ge(exp_done, u)
                                tgt, new = tgt2[:, q:q + 1], new2[:, q]
                                lo, hi = ends2[:, q, 0], ends2[:, q, 1]
                                dve.wait_ge(bracketed, u)
                                for k in range(EVALS[step]):
                                    if k > 0:
                                        then(V_.tensor_tensor(sc[:, 1:2], hi[:, 1:2], lo[:, 1:2], ALU.subtract),
                                             V_.tensor_tensor(sc[:, 2:3], hi[:, 0:1], lo[:, 1:2], ALU.mult))
                                        then(V_.reciprocal(sc[:, 4:5], sc[:, 1:2]),
                                             V_.scalar_tensor_tensor(out=sc[:, 3:4], in0=lo[:, 0:1], scalar=hi[:, 1:2],
                                                                     in1=sc[:, 2:3], op0=ALU.mult, op1=ALU.subtract))
                                        then(V_.tensor_scalar(new[:, 0:1], sc[:, 3:4], sc[:, 4:5], hi[:, 0:1], ALU.mult, ALU.min))
                                    then(V_.tensor_scalar(sc[:, 0:1], new[:, 0:1], AIM, tgt, ALU.mult, ALU.subtract),
                                         V_.tensor_scalar(lo[:, 1:2], lo[:, 1:2], KEEP_END, None, ALU.mult),
                                         V_.tensor_scalar(hi[:, 1:2], hi[:, 1:2], KEEP_END, None, ALU.mult),
                                         V_.scalar_tensor_tensor(out=U[:, 0:N], in0=e, scalar=new[:, 0:1], in1=e,
                                                                 op0=ALU.is_ge, op1=ALU.mult, accum_out=new[:, 2:3]))
                                    then(V_.tensor_tensor(new[:, 1:2], new[:, 2:3], sc[:, 0:1], ALU.add),
                                         V_.tensor_scalar(up[:], new[:, 2:3].to_broadcast([P, 3]), tgt, None, ALU.is_ge),
                                         V_.tensor_scalar(down[:], new[:, 2:3].to_broadcast([P, 3]), tgt, None, ALU.is_lt))
                                    then(V_.copy_predicated(lo, up[:], new), V_.copy_predicated(hi, down[:], new))
                                    if k == MAX_AFTER[step] and live[0]:
                                        row_max()
                                then(V_.scalar_tensor_tensor(out=U[:, 0:N], in0=e, scalar=hi[:, 0:1], in1=e,
                                                             op0=ALU.is_ge, op1=ALU.subtract, reverse1=True),
                                     V_.tensor_copy(mass[:, 0:1], hi[:, 2:3]))
                                dve.reg_mov(more, 1)
                                with dve.Fori(0, more):
                                    dve.sem_clear(rnd)
                                    m = [0]

                                    def rthen(*ins):
                                        for i in ins:
                                            i.then_inc(rnd, 1)
                                        m[0] += len(ins)
                                        dve.wait_ge(rnd, m[0])
                                    rthen(V_.memset(U[:, N:NPAD], MARK_PAD), V_.memset(mark[:], MARK_PAD),
                                          V_.max(top8[:], U[:, 0:N]))
                                    rthen(V_.tensor_tensor_scan(mass[:, 1:TOP + 1], ones8[:], top8[:], mass[:, 0:1],
                                                                ALU.mult, ALU.add))
                                    rthen(V_.tensor_scalar(flag[:, 0:1], mass[:, TOP:TOP + 1], tgt, None, ALU.is_lt),
                                          V_.tensor_scalar(keep[:], mass[:, 0:TOP], tgt, None, ALU.is_lt),
                                          V_.scalar_tensor_tensor(out=kmass[:], in0=mass[:, 0:TOP], scalar=tgt,
                                                                  in1=mass[:, 1:TOP + 1], op0=ALU.is_lt, op1=ALU.mult))
                                    rthen(V_.transpose(flagT[:], flag[:]),
                                          V_.copy_predicated(mark[:], keep[:], top8[:]),
                                          V_.reduce_max(sc[:, 6:7], kmass[:], axis=AX_X))
                                    rthen(V_.reduce_max(flagm[:], flagT[:], axis=AX_X),
                                          V_.tensor_tensor(mass[:, 0:1], mass[:, 0:1], sc[:, 6:7], ALU.max))
                                    rthen(V_.tensor_copy(flagi[:], flagm[:]))
                                    V_.match_replace(U[:], mark[:], U[:], MARKED).then_inc(rnd, 1)
                                    for i in range(4):
                                        dve.reg_load(open_rows[i], flagi[32 * i:32 * i + 1, 0:1])
                                    dve.reg_add(open_rows[0], open_rows[0], open_rows[1])
                                    dve.reg_add(open_rows[2], open_rows[2], open_rows[3])
                                    dve.reg_add(open_rows[0], open_rows[0], open_rows[2])
                                    dve.reg_alu(open_rows[0], open_rows[0], NP, ALU.mult)
                                    dve.reg_mov(more, open_rows[0])
                                    m[0] += 1
                                    dve.wait_ge(rnd, m[0])
                                if later(u, 3):
                                    dve.wait_ge(xa_ready if step == 0 else ax_copied, u - 2)
                                V_.reciprocal(rz[:, q:q + 1], mass[:, 0:1]).then_inc(search, 1)
                                V_.scalar_tensor_tensor(out=e, in0=U[:, 0:N], scalar=0.0, in1=e,
                                                        op0=ALU.is_le, op1=ALU.mult).then_inc(search, 1)
                                V_.memset(E[:, q, N:NP], 0.0).then_inc(search, 1)
                                dve.wait_ge(search, count[0] + 3)
                                dve.sem_inc(probs_ready, 1)
                                dve.sem_inc(searched, 1)
                            pipeline(dve, NT, body)

        layer("operand3", x3_t, nxt="dense", weight=Wg3, hnext=Ha)
        layer("layer3", x3_t, rhs=Ha, plus_self=False, evac="layer3",
              dst_t=out.rearrange("(t p) c -> t p c", p=P))


def kernel(**inputs):
    from concourse import bacc
    from concourse.bass_utils import run_bass_kernel_spmd

    x = np.asarray(inputs["x"])
    adj = np.asarray(inputs["adj"])
    n, d = x.shape
    nt = -(-n // P)
    nt += nt % 2
    n_pad = nt * P
    xp = np.zeros((n_pad, d), np.float32)
    xp[:n] = x
    ap = np.zeros((n_pad, n_pad), np.float32)
    ap[:n, :n] = adj
    adjT = np.ascontiguousarray(ap.reshape(nt, P, nt, P).transpose(0, 3, 2, 1))
    w = {k: np.asarray(v) for k, v in inputs.items()}
    side = lambda a, b: np.ascontiguousarray(np.concatenate([a, b], axis=1))
    U1, U2, U3 = w["L2_gnn_U1"], w["L2_gnn_U2"], w["L2_gnn_U3"]
    arrays = {
        "xin": xp, "adjR": ap.reshape(nt, P, n_pad), "adjT": adjT, "W0T": np.ascontiguousarray(w["L0_gnn_W"].T), "b0": w["L0_gnn_b"],
        "W1g": w["L1_gnn_weight"], "A1T": np.ascontiguousarray(w["L2_gnn_W1"].T), "A2": w["L2_gnn_W2"],
        "A3": w["L2_gnn_W3"], "UA": side(U1[0], U2[0]), "UB": side(U1[1], U2[1]), "UC": side(U3[0], U3[1]),
        "gamma": w["L2_gnn_gamma"], "beta": w["L2_gnn_beta"], "tin": w["L3_gnn_t"], "Wg3": w["L3_gnn_weight"],
    }
    nc = bacc.Bacc("TRN2", target_bir_lowering=False, num_devices=1)
    args = {k: nc.dram_tensor(k, a.shape, mybir.dt.from_np(a.dtype), kind="ExternalInput").ap()
            for k, a in arrays.items()}
    out = nc.dram_tensor("out", (n_pad, d), F32, kind="ExternalOutput").ap()
    build(nc, n, out=out, **args)
    r = run_bass_kernel_spmd(nc, [arrays], core_ids=[0])
    return r.results[0]["out"][:n]
```
